# Optimizing a Trainium2 kernel written in Bass

```python
import numpy as np
import jax
import jax.numpy as jnp

def _softmax(x, axis=-1):
    return jax.nn.softmax(x, axis=axis)

def _gelu(x):
    return jax.nn.gelu(x, approximate=True)

def _silu(x):
    return jax.nn.silu(x)

def _sigmoid(x):
    return jax.nn.sigmoid(x)

def _layernorm(x, axis=-1, eps=1e-05):
    m = jnp.mean(x, axis=axis, keepdims=True)
    v = jnp.var(x, axis=axis, keepdims=True)
    return (x - m) / jnp.sqrt(v + eps)

def _scatter_add(tgt, idx, src, axis=0):
    return tgt.at[idx].add(src)

def _segment_sum(src, seg, n):
    return jax.ops.segment_sum(src, seg, n)
kernel_name = 'mk_pixart_resid_d4_seqx_r8_feb471'

def setup_inputs(seed: int=0):
    np.random.seed(seed)
    _w = jnp.asarray

    def _rec_inputs():
        import jax
        import jax.numpy as jnp
        _rk = jax.random.key(seed)
        x = -0.003379 + 0.9984 * jax.random.normal(jax.random.fold_in(_rk, 1), (2, 512, 128), jnp.float32)
        _lenS = 512 - jax.random.randint(jax.random.fold_in(_rk, 7), (2,), 0, max(1, 512 // 4) + 1, jnp.int32)
        _lenS2 = 154 - jax.random.randint(jax.random.fold_in(_rk, 8), (2,), 0, max(1, 154 // 4) + 1, jnp.int32)
        cond_1024 = -0.0142567 + 1.00875 * jax.random.normal(jax.random.fold_in(_rk, 11), (2, 128), jnp.float32)
        _ctx_1024P = jax.random.normal(jax.random.fold_in(_rk, 12), (2, 16, 128), jnp.float32)
        _ctx_1024c = jax.random.dirichlet(jax.random.fold_in(_rk, 512), 0.3 * jnp.ones((16,), jnp.float32), (2, 154))
        _ctx_1024t = jnp.einsum('bsk,bkd->bsd', _ctx_1024c, _ctx_1024P)
        _ctx_1024t = _ctx_1024t * jax.lax.rsqrt(jnp.mean(jnp.square(_ctx_1024t)) + 1e-12) * 0.953939
        ctx_1024 = -5.72187e-05 + 0.999849 * (_ctx_1024t + 0.3 * jax.random.normal(jax.random.fold_in(_rk, 612), (2, 154, 128), jnp.float32))
        _validS = jnp.arange(512)[None, :] < _lenS[:, None]
        _validS2 = jnp.arange(154)[None, :] < _lenS2[:, None]
        _causal = jnp.tril(jnp.ones((512, 512), dtype=bool))
        mask_BxS_bf0 = jnp.logical_not(jnp.ones((2, 512), dtype=bool))
        mask_BxS2_bf0 = jnp.logical_not(jnp.ones((2, 154), dtype=bool))
        return (x, cond_1024, ctx_1024, mask_BxS_bf0, mask_BxS2_bf0)
    x, cond_1024, ctx_1024, mask_BxS_bf0, mask_BxS2_bf0 = _rec_inputs()

    def _L0_xcond_setup():
        import jax, jax.numpy as jnp
        import numpy as np
        B, N, K, D, T = (16, 512, 16, 128, 3)
        EPS_ATTN = 1e-08
        LN_EPS = 1e-05

        def _ln(x, g, b):
            mu = jnp.mean(x, axis=-1, keepdims=True)
            var = jnp.mean(jnp.square(x - mu), axis=-1, keepdims=True)
            return (x - mu) * jax.lax.rsqrt(var + LN_EPS) * g + b
        key = jax.random.key(seed)
        ks = jax.random.split(key, 16)
        w = lambda k, i, o: jax.random.normal(k, (i, o), jnp.float32) * 0.02
        inp = {'x_cls': jax.random.normal(ks[0], (B, D), jnp.float32), 'x': jax.random.normal(ks[1], (B, N, D), jnp.float32), 'noise': jax.random.normal(ks[2], (B, K, D), jnp.float32), 'q_mu': jax.random.normal(ks[3], (1, 1, D), jnp.float32), 'q_logsig': jax.random.normal(ks[4], (1, 1, D), jnp.float32) * 0.02, 'lnkv_g': jnp.ones((D,), jnp.float32), 'lnkv_b': jnp.zeros((D,), jnp.float32), 'lnq_g': jnp.ones((D,), jnp.float32), 'lnq_b': jnp.zeros((D,), jnp.float32), 'lnm_g': jnp.ones((D,), jnp.float32), 'lnm_b': jnp.zeros((D,), jnp.float32), 'lnp_g': jnp.ones((D,), jnp.float32), 'lnp_b': jnp.zeros((D,), jnp.float32), 'wk': w(ks[5], D, D), 'bk': jnp.zeros((D,), jnp.float32), 'wv': w(ks[6], D, D), 'bv': jnp.zeros((D,), jnp.float32), 'wq': w(ks[7], D, D), 'bq': jnp.zeros((D,), jnp.float32), 'wu': w(ks[8], D, D), 'bu': jnp.zeros((D,), jnp.float32), 'w1': w(ks[9], D, D), 'b1': jnp.zeros((D,), jnp.float32), 'w2': w(ks[10], D, D), 'b2': jnp.zeros((D,), jnp.float32)}
        return inp
    _L0_xcond_all = _L0_xcond_setup()
    _L0_xcond_in = {k: v for k, v in _L0_xcond_all.items() if k in ('q_mu', 'q_logsig', 'lnkv_g', 'lnkv_b', 'lnq_g', 'lnq_b', 'lnm_g', 'lnm_b', 'lnp_g', 'lnp_b', 'wk', 'bk', 'wv', 'bv', 'wq', 'bq', 'wu', 'bu', 'w1', 'b1', 'w2', 'b2')}
    del _L0_xcond_all

    def _L0_ffn_setup():
        import jax, jax.numpy as jnp
        import numpy as np
        HIDDEN = 128
        NUM_EXPERTS = 8
        TOP_K = 2
        FFN = 512
        BATCH, SEQ = (4, 256)
        key = jax.random.key(seed)
        k_x, k_r, k_w1, k_w2 = jax.random.split(key, 4)
        x = jax.random.normal(k_x, (BATCH, SEQ, HIDDEN), dtype=jnp.float32)
        router_w = jax.random.normal(k_r, (NUM_EXPERTS, HIDDEN), dtype=jnp.float32) * (1.0 / np.sqrt(HIDDEN))
        lim = float(np.sqrt(6.0 / (FFN + HIDDEN)))
        expert_w1 = jax.random.uniform(k_w1, (NUM_EXPERTS, FFN, HIDDEN), dtype=jnp.float32, minval=-lim, maxval=lim)
        expert_w2 = jax.random.uniform(k_w2, (NUM_EXPERTS, HIDDEN, FFN), dtype=jnp.float32, minval=-lim, maxval=lim)
        return {'x': x, 'router_w': router_w, 'expert_w1': expert_w1, 'expert_w2': expert_w2}
    _L0_ffn_all = _L0_ffn_setup()
    _L0_ffn_in = {k: v for k, v in _L0_ffn_all.items() if k in ('router_w', 'expert_w1', 'expert_w2')}
    del _L0_ffn_all

    def _L1_xcond_setup():
        import jax, jax.numpy as jnp
        import numpy as np
        DIM = 128
        DIM_HEAD = 64
        HEADS = 16
        INNER = DIM_HEAD * HEADS
        B, N1, N2 = (8, 512, 32)
        EPS = 1e-05

        def layer_norm(x, w, b):
            mu = jnp.mean(x, axis=-1, keepdims=True)
            var = jnp.var(x, axis=-1, keepdims=True)
            return (x - mu) * jax.lax.rsqrt(var + EPS) * w + b
        key = jax.random.key(seed)
        ks = jax.random.split(key, 10)
        return {'x': jax.random.normal(ks[0], (B, N1, DIM), jnp.float32), 'latents': jax.random.normal(ks[1], (B, N2, DIM), jnp.float32), 'shift': jax.random.normal(ks[2], (B, DIM), jnp.float32), 'scale': jax.random.normal(ks[3], (B, DIM), jnp.float32), 'ln1_w': jnp.ones((DIM,), jnp.float32), 'ln1_b': jnp.zeros((DIM,), jnp.float32), 'ln2_w': jnp.ones((DIM,), jnp.float32), 'ln2_b': jnp.zeros((DIM,), jnp.float32), 'Wq': jax.random.normal(ks[4], (INNER, DIM), jnp.float32) * 0.02, 'Wkv': jax.random.normal(ks[5], (2 * INNER, DIM), jnp.float32) * 0.02, 'Wo': jax.random.normal(ks[6], (DIM, INNER), jnp.float32) * 0.02}
    _L1_xcond_all = _L1_xcond_setup()
    _L1_xcond_in = {k: v for k, v in _L1_xcond_all.items() if k in ('ln1_w', 'ln1_b', 'ln2_w', 'ln2_b', 'Wq', 'Wkv', 'Wo')}
    del _L1_xcond_all

    def _L1_ffn_setup():
        import jax, jax.numpy as jnp
        import numpy as np
        B, S, D, F, E, R = (4, 256, 128, 512, 8, 4)
        key = jax.random.key(seed)
        ks = jax.random.split(key, 8)
        s_in = 1.0 / np.sqrt(D)
        s_ff = 1.0 / np.sqrt(F)
        return {'hidden_states': jax.random.normal(ks[0], (B, S, D), jnp.float32), 'gate_W': jax.random.normal(ks[1], (E, D), jnp.float32) * s_in, 'gate_b': jnp.zeros((E,), jnp.float32), 'wi_W': jax.random.normal(ks[2], (F, D), jnp.float32) * s_in, 'wi_b': jnp.zeros((F,), jnp.float32), 'wo_W': jax.random.normal(ks[3], (D, F), jnp.float32) * s_ff, 'wo_b': jnp.zeros((D,), jnp.float32), 'lora_A': jax.random.normal(ks[4], (E, R, D), jnp.float32) * s_in, 'lora_B': jax.random.normal(ks[5], (E, F, R), jnp.float32) * 0.02}
    _L1_ffn_all = _L1_ffn_setup()
    _L1_ffn_in = {k: v for k, v in _L1_ffn_all.items() if k in ('gate_W', 'gate_b', 'wi_W', 'wi_b', 'wo_W', 'wo_b', 'lora_A', 'lora_B')}
    del _L1_ffn_all

    def _L2_xcond_setup():
        import jax, jax.numpy as jnp
        import numpy as np
        NL, D, H, DFF = (6, 128, 16, 512)
        HD = D // H

        def _rope(x):
            L = x.shape[1]
            half = HD // 2
            inv = 1.0 / 10000.0 ** (jnp.arange(half, dtype=jnp.float32) / half)
            ang = jnp.arange(L, dtype=jnp.float32)[:, None] * inv
            cos = jnp.cos(ang)[None, :, None, :]
            sin = jnp.sin(ang)[None, :, None, :]
            x1, x2 = (x[..., :half], x[..., half:])
            return jnp.concatenate([x1 * cos - x2 * sin, x1 * sin + x2 * cos], axis=-1)

        def _ln(x, eps=1e-05):
            m = jnp.mean(x, axis=-1, keepdims=True)
            v = jnp.var(x, axis=-1, keepdims=True)
            return (x - m) * jax.lax.rsqrt(v + eps)

        def _adaln(x, emb, w, b):
            gb = emb[:, 0, :] @ w.T + b
            g, be = jnp.split(gb, 2, axis=-1)
            return _ln(x) * (1.0 + g[:, None, :]) + be[:, None, :]

        def _attn(q, k, v, mask):
            scores = jnp.einsum('bqhd,bkhd->bhqk', q, k) / np.float32(np.sqrt(HD))
            scores = jnp.where(mask[:, None, None, :], jnp.float32(-jnp.inf), scores)
            w = jax.nn.softmax(scores, axis=-1)
            return jnp.einsum('bhqk,bkhd->bqhd', w, v)
        key = jax.random.key(seed)
        ks = jax.random.split(key, 20)
        B, L, LC = (4, 128, 64)
        s = 0.02
        inp = {'x': jax.random.normal(ks[0], (B, L, D), jnp.float32), 'noise_emb': jax.random.normal(ks[1], (B, 1, D), jnp.float32), 'context': jax.random.normal(ks[2], (B, LC, D), jnp.float32), 'src_mask': jnp.zeros((B, L), bool), 'ctx_mask': jnp.zeros((B, LC), bool), 'n1_w': jax.random.normal(ks[3], (NL, 2 * D, D), jnp.float32) * s, 'n1_b': jnp.zeros((NL, 2 * D), jnp.float32), 'n2_w': jax.random.normal(ks[4], (NL, 2 * D, D), jnp.float32) * s, 'n2_b': jnp.zeros((NL, 2 * D), jnp.float32), 'n3_w': jax.random.normal(ks[5], (NL, 2 * D, D), jnp.float32) * s, 'n3_b': jnp.zeros((NL, 2 * D), jnp.float32), 'qkv_w': jax.random.normal(ks[6], (NL, 3 * D, D), jnp.float32) * s, 'so_w': jax.random.normal(ks[7], (NL, D, D), jnp.float32) * s, 'cq_w': jax.random.normal(ks[8], (NL, D, D), jnp.float32) * s, 'ck_w': jax.random.normal(ks[9], (NL, D, D), jnp.float32) * s, 'cv_w': jax.random.normal(ks[10], (NL, D, D), jnp.float32) * s, 'co_w': jax.random.normal(ks[11], (NL, D, D), jnp.float32) * s, 'f1_w': jax.random.normal(ks[12], (NL, DFF, D), jnp.float32) * s, 'f1_b': jnp.zeros((NL, DFF), jnp.float32), 'f2_w': jax.random.normal(ks[13], (NL, D, DFF), jnp.float32) * s, 'f2_b': jnp.zeros((NL, D), jnp.float32)}
        return inp
    _L2_xcond_all = _L2_xcond_setup()
    _L2_xcond_in = {k: v for k, v in _L2_xcond_all.items() if k in ('n1_w', 'n1_b', 'n2_w', 'n2_b', 'n3_w', 'n3_b', 'qkv_w', 'so_w', 'cq_w', 'ck_w', 'cv_w', 'co_w', 'f1_w', 'f1_b', 'f2_w', 'f2_b')}
    del _L2_xcond_all

    def _L2_ffn_setup():
        import jax, jax.numpy as jnp
        import numpy as np
        BLOCK = 32
        W_BITS = 4
        ACT_BITS = 16

        def act_qdq(x):
            qmax = 2.0 ** (ACT_BITS - 1) - 1.0
            scale = jnp.maximum(jnp.max(jnp.abs(x)) / qmax, 1e-12)
            return jnp.clip(jnp.round(x / scale), -qmax - 1.0, qmax) * scale

        def fixed_qdq_u16(x):
            scale = 1.0 / 65536.0
            return jnp.clip(jnp.round(x / scale), 0.0, 65535.0) * scale

        def lpbq_dequant(w):
            O, I = w.shape
            qmax = 2.0 ** (W_BITS - 1) - 1.0
            wb = w.reshape(O, I // BLOCK, BLOCK)
            s = jnp.maximum(jnp.max(jnp.abs(wb), axis=-1, keepdims=True) / qmax, 1e-12)
            wq = jnp.clip(jnp.round(wb / s), -qmax - 1.0, qmax) * s
            return wq.reshape(O, I)
        key = jax.random.key(seed)
        k1, k2, k3, k4 = jax.random.split(key, 4)
        B, S, H, I = (2, 512, 128, 384)
        x = jax.random.normal(k1, (B, S, H), jnp.float32)
        w_gate = jax.random.normal(k2, (I, H), jnp.float32) * 0.02
        w_up = jax.random.normal(k3, (I, H), jnp.float32) * 0.02
        w_down = jax.random.normal(k4, (H, I), jnp.float32) * 0.02
        return {'x': x, 'w_gate': w_gate, 'w_up': w_up, 'w_down': w_down}
    _L2_ffn_all = _L2_ffn_setup()
    _L2_ffn_in = {k: v for k, v in _L2_ffn_all.items() if k in ('w_gate', 'w_up', 'w_down')}
    del _L2_ffn_all

    def _L3_xcond_setup():
        import jax, jax.numpy as jnp
        import numpy as np
        NL, D, H, DFF = (6, 128, 16, 512)
        HD = D // H

        def _rope(x):
            L = x.shape[1]
            half = HD // 2
            inv = 1.0 / 10000.0 ** (jnp.arange(half, dtype=jnp.float32) / half)
            ang = jnp.arange(L, dtype=jnp.float32)[:, None] * inv
            cos = jnp.cos(ang)[None, :, None, :]
            sin = jnp.sin(ang)[None, :, None, :]
            x1, x2 = (x[..., :half], x[..., half:])
            return jnp.concatenate([x1 * cos - x2 * sin, x1 * sin + x2 * cos], axis=-1)

        def _ln(x, eps=1e-05):
            m = jnp.mean(x, axis=-1, keepdims=True)
            v = jnp.var(x, axis=-1, keepdims=True)
            return (x - m) * jax.lax.rsqrt(v + eps)

        def _adaln(x, emb, w, b):
            gb = emb[:, 0, :] @ w.T + b
            g, be = jnp.split(gb, 2, axis=-1)
            return _ln(x) * (1.0 + g[:, None, :]) + be[:, None, :]

        def _attn(q, k, v, mask):
            scores = jnp.einsum('bqhd,bkhd->bhqk', q, k) / np.float32(np.sqrt(HD))
            scores = jnp.where(mask[:, None, None, :], jnp.float32(-jnp.inf), scores)
            w = jax.nn.softmax(scores, axis=-1)
            return jnp.einsum('bhqk,bkhd->bqhd', w, v)
        key = jax.random.key(seed)
        ks = jax.random.split(key, 20)
        B, L, LC = (4, 128, 64)
        s = 0.02
        inp = {'x': jax.random.normal(ks[0], (B, L, D), jnp.float32), 'noise_emb': jax.random.normal(ks[1], (B, 1, D), jnp.float32), 'context': jax.random.normal(ks[2], (B, LC, D), jnp.float32), 'src_mask': jnp.zeros((B, L), bool), 'ctx_mask': jnp.zeros((B, LC), bool), 'n1_w': jax.random.normal(ks[3], (NL, 2 * D, D), jnp.float32) * s, 'n1_b': jnp.zeros((NL, 2 * D), jnp.float32), 'n2_w': jax.random.normal(ks[4], (NL, 2 * D, D), jnp.float32) * s, 'n2_b': jnp.zeros((NL, 2 * D), jnp.float32), 'n3_w': jax.random.normal(ks[5], (NL, 2 * D, D), jnp.float32) * s, 'n3_b': jnp.zeros((NL, 2 * D), jnp.float32), 'qkv_w': jax.random.normal(ks[6], (NL, 3 * D, D), jnp.float32) * s, 'so_w': jax.random.normal(ks[7], (NL, D, D), jnp.float32) * s, 'cq_w': jax.random.normal(ks[8], (NL, D, D), jnp.float32) * s, 'ck_w': jax.random.normal(ks[9], (NL, D, D), jnp.float32) * s, 'cv_w': jax.random.normal(ks[10], (NL, D, D), jnp.float32) * s, 'co_w': jax.random.normal(ks[11], (NL, D, D), jnp.float32) * s, 'f1_w': jax.random.normal(ks[12], (NL, DFF, D), jnp.float32) * s, 'f1_b': jnp.zeros((NL, DFF), jnp.float32), 'f2_w': jax.random.normal(ks[13], (NL, D, DFF), jnp.float32) * s, 'f2_b': jnp.zeros((NL, D), jnp.float32)}
        return inp
    _L3_xcond_all = _L3_xcond_setup()
    _L3_xcond_in = {k: v for k, v in _L3_xcond_all.items() if k in ('n1_w', 'n1_b', 'n2_w', 'n2_b', 'n3_w', 'n3_b', 'qkv_w', 'so_w', 'cq_w', 'ck_w', 'cv_w', 'co_w', 'f1_w', 'f1_b', 'f2_w', 'f2_b')}
    del _L3_xcond_all

    def _L3_ffn_setup():
        import jax, jax.numpy as jnp
        import numpy as np
        B, N, D, E, DFF = (4, 256, 128, 16, 512)
        CAPACITY_FACTOR = 2.0
        CAP = int(N * CAPACITY_FACTOR / E)
        SINKHORN_ITERS = 6

        def _sinkhorn(logits, n_iters=SINKHORN_ITERS, tau=1.0):
            t = logits / tau
            for _ in range(n_iters):
                t = t - jax.scipy.special.logsumexp(t, axis=-2, keepdims=True)
                t = t - jax.scipy.special.logsumexp(t, axis=-1, keepdims=True)
            return jnp.exp(t)
        key = jax.random.key(seed)
        ks = jax.random.split(key, 6)
        scaled = lambda k, sh, fan: (jax.random.normal(k, sh, jnp.float32) / np.sqrt(fan)).astype(jnp.float32)
        return {'x': jax.random.normal(ks[0], (B, N, D), jnp.float32), 'gate_query': scaled(ks[1], (E, D), D), 'log_temp': jnp.asarray(np.log(0.5), jnp.float32), 'w1': scaled(ks[2], (E, D, DFF), D), 'b1': jnp.zeros((E, DFF), jnp.float32), 'w2': scaled(ks[3], (E, DFF, D), DFF), 'b2': jnp.zeros((E, D), jnp.float32)}
    _L3_ffn_all = _L3_ffn_setup()
    _L3_ffn_in = {k: v for k, v in _L3_ffn_all.items() if k in ('gate_query', 'log_temp', 'w1', 'b1', 'w2', 'b2')}
    del _L3_ffn_all
    return {'x': x, 'cond_1024': cond_1024, 'ctx_1024': ctx_1024, 'mask_BxS_bf0': mask_BxS_bf0, 'mask_BxS2_bf0': mask_BxS2_bf0, 'L0_xcond_q_mu': _L0_xcond_in['q_mu'], 'L0_xcond_q_logsig': _L0_xcond_in['q_logsig'], 'L0_xcond_lnkv_g': _L0_xcond_in['lnkv_g'], 'L0_xcond_lnkv_b': _L0_xcond_in['lnkv_b'], 'L0_xcond_lnq_g': _L0_xcond_in['lnq_g'], 'L0_xcond_lnq_b': _L0_xcond_in['lnq_b'], 'L0_xcond_lnm_g': _L0_xcond_in['lnm_g'], 'L0_xcond_lnm_b': _L0_xcond_in['lnm_b'], 'L0_xcond_lnp_g': _L0_xcond_in['lnp_g'], 'L0_xcond_lnp_b': _L0_xcond_in['lnp_b'], 'L0_xcond_wk': _L0_xcond_in['wk'], 'L0_xcond_bk': _L0_xcond_in['bk'], 'L0_xcond_wv': _L0_xcond_in['wv'], 'L0_xcond_bv': _L0_xcond_in['bv'], 'L0_xcond_wq': _L0_xcond_in['wq'], 'L0_xcond_bq': _L0_xcond_in['bq'], 'L0_xcond_wu': _L0_xcond_in['wu'], 'L0_xcond_bu': _L0_xcond_in['bu'], 'L0_xcond_w1': _L0_xcond_in['w1'], 'L0_xcond_b1': _L0_xcond_in['b1'], 'L0_xcond_w2': _L0_xcond_in['w2'], 'L0_xcond_b2': _L0_xcond_in['b2'], 'L0_ffn_router_w': _L0_ffn_in['router_w'], 'L0_ffn_expert_w1': _L0_ffn_in['expert_w1'], 'L0_ffn_expert_w2': _L0_ffn_in['expert_w2'], 'L1_xcond_ln1_w': _L1_xcond_in['ln1_w'], 'L1_xcond_ln1_b': _L1_xcond_in['ln1_b'], 'L1_xcond_ln2_w': _L1_xcond_in['ln2_w'], 'L1_xcond_ln2_b': _L1_xcond_in['ln2_b'], 'L1_xcond_Wq': _L1_xcond_in['Wq'], 'L1_xcond_Wkv': _L1_xcond_in['Wkv'], 'L1_xcond_Wo': _L1_xcond_in['Wo'], 'L1_ffn_gate_W': _L1_ffn_in['gate_W'], 'L1_ffn_gate_b': _L1_ffn_in['gate_b'], 'L1_ffn_wi_W': _L1_ffn_in['wi_W'], 'L1_ffn_wi_b': _L1_ffn_in['wi_b'], 'L1_ffn_wo_W': _L1_ffn_in['wo_W'], 'L1_ffn_wo_b': _L1_ffn_in['wo_b'], 'L1_ffn_lora_A': _L1_ffn_in['lora_A'], 'L1_ffn_lora_B': _L1_ffn_in['lora_B'], 'L2_xcond_n1_w': _L2_xcond_in['n1_w'], 'L2_xcond_n1_b': _L2_xcond_in['n1_b'], 'L2_xcond_n2_w': _L2_xcond_in['n2_w'], 'L2_xcond_n2_b': _L2_xcond_in['n2_b'], 'L2_xcond_n3_w': _L2_xcond_in['n3_w'], 'L2_xcond_n3_b': _L2_xcond_in['n3_b'], 'L2_xcond_qkv_w': _L2_xcond_in['qkv_w'], 'L2_xcond_so_w': _L2_xcond_in['so_w'], 'L2_xcond_cq_w': _L2_xcond_in['cq_w'], 'L2_xcond_ck_w': _L2_xcond_in['ck_w'], 'L2_xcond_cv_w': _L2_xcond_in['cv_w'], 'L2_xcond_co_w': _L2_xcond_in['co_w'], 'L2_xcond_f1_w': _L2_xcond_in['f1_w'], 'L2_xcond_f1_b': _L2_xcond_in['f1_b'], 'L2_xcond_f2_w': _L2_xcond_in['f2_w'], 'L2_xcond_f2_b': _L2_xcond_in['f2_b'], 'L2_ffn_w_gate': _L2_ffn_in['w_gate'], 'L2_ffn_w_up': _L2_ffn_in['w_up'], 'L2_ffn_w_down': _L2_ffn_in['w_down'], 'L3_xcond_n1_w': _L3_xcond_in['n1_w'], 'L3_xcond_n1_b': _L3_xcond_in['n1_b'], 'L3_xcond_n2_w': _L3_xcond_in['n2_w'], 'L3_xcond_n2_b': _L3_xcond_in['n2_b'], 'L3_xcond_n3_w': _L3_xcond_in['n3_w'], 'L3_xcond_n3_b': _L3_xcond_in['n3_b'], 'L3_xcond_qkv_w': _L3_xcond_in['qkv_w'], 'L3_xcond_so_w': _L3_xcond_in['so_w'], 'L3_xcond_cq_w': _L3_xcond_in['cq_w'], 'L3_xcond_ck_w': _L3_xcond_in['ck_w'], 'L3_xcond_cv_w': _L3_xcond_in['cv_w'], 'L3_xcond_co_w': _L3_xcond_in['co_w'], 'L3_xcond_f1_w': _L3_xcond_in['f1_w'], 'L3_xcond_f1_b': _L3_xcond_in['f1_b'], 'L3_xcond_f2_w': _L3_xcond_in['f2_w'], 'L3_xcond_f2_b': _L3_xcond_in['f2_b'], 'L3_ffn_gate_query': _L3_ffn_in['gate_query'], 'L3_ffn_log_temp': _L3_ffn_in['log_temp'], 'L3_ffn_w1': _L3_ffn_in['w1'], 'L3_ffn_b1': _L3_ffn_in['b1'], 'L3_ffn_w2': _L3_ffn_in['w2'], 'L3_ffn_b2': _L3_ffn_in['b2']}

def reference(x, cond_1024, ctx_1024, mask_BxS_bf0, mask_BxS2_bf0, L0_xcond_q_mu, L0_xcond_q_logsig, L0_xcond_lnkv_g, L0_xcond_lnkv_b, L0_xcond_lnq_g, L0_xcond_lnq_b, L0_xcond_lnm_g, L0_xcond_lnm_b, L0_xcond_lnp_g, L0_xcond_lnp_b, L0_xcond_wk, L0_xcond_bk, L0_xcond_wv, L0_xcond_bv, L0_xcond_wq, L0_xcond_bq, L0_xcond_wu, L0_xcond_bu, L0_xcond_w1, L0_xcond_b1, L0_xcond_w2, L0_xcond_b2, L0_ffn_router_w, L0_ffn_expert_w1, L0_ffn_expert_w2, L1_xcond_ln1_w, L1_xcond_ln1_b, L1_xcond_ln2_w, L1_xcond_ln2_b, L1_xcond_Wq, L1_xcond_Wkv, L1_xcond_Wo, L1_ffn_gate_W, L1_ffn_gate_b, L1_ffn_wi_W, L1_ffn_wi_b, L1_ffn_wo_W, L1_ffn_wo_b, L1_ffn_lora_A, L1_ffn_lora_B, L2_xcond_n1_w, L2_xcond_n1_b, L2_xcond_n2_w, L2_xcond_n2_b, L2_xcond_n3_w, L2_xcond_n3_b, L2_xcond_qkv_w, L2_xcond_so_w, L2_xcond_cq_w, L2_xcond_ck_w, L2_xcond_cv_w, L2_xcond_co_w, L2_xcond_f1_w, L2_xcond_f1_b, L2_xcond_f2_w, L2_xcond_f2_b, L2_ffn_w_gate, L2_ffn_w_up, L2_ffn_w_down, L3_xcond_n1_w, L3_xcond_n1_b, L3_xcond_n2_w, L3_xcond_n2_b, L3_xcond_n3_w, L3_xcond_n3_b, L3_xcond_qkv_w, L3_xcond_so_w, L3_xcond_cq_w, L3_xcond_ck_w, L3_xcond_cv_w, L3_xcond_co_w, L3_xcond_f1_w, L3_xcond_f1_b, L3_xcond_f2_w, L3_xcond_f2_b, L3_ffn_gate_query, L3_ffn_log_temp, L3_ffn_w1, L3_ffn_b1, L3_ffn_w2, L3_ffn_b2):
    import jax
    import jax.numpy as jnp

    def _L0_xcond_ref(x_cls, x, noise, q_mu, q_logsig, lnkv_g, lnkv_b, lnq_g, lnq_b, lnm_g, lnm_b, lnp_g, lnp_b, wk, bk, wv, bv, wq, bq, wu, bu, w1, b1, w2, b2):
        import jax, jax.numpy as jnp
        import numpy as np
        B, N, K, D, T = (16, 512, 16, 128, 3)
        EPS_ATTN = 1e-08
        LN_EPS = 1e-05

        def _ln(x, g, b):
            mu = jnp.mean(x, axis=-1, keepdims=True)
            var = jnp.mean(jnp.square(x - mu), axis=-1, keepdims=True)
            return (x - mu) * jax.lax.rsqrt(var + LN_EPS) * g + b
        scale = D ** (-0.5)
        x_in = _ln(x, lnkv_g, lnkv_b)
        k = x_in @ wk + bk
        v = x_in @ wv + bv
        slots = q_mu + jnp.exp(q_logsig) * noise
        for _ in range(T):
            prev = slots
            q = _ln(slots, lnq_g, lnq_b) @ wq + bq
            logits = jnp.einsum('bnd,bkd->bnk', k, q) / scale
            attn = jax.nn.softmax(logits, axis=-1) + EPS_ATTN
            attn = attn / jnp.sum(attn, axis=1, keepdims=True)
            upd = jnp.einsum('bnk,bnd->bkd', attn, v)
            slots = upd @ wu + bu + prev
            h = _ln(slots, lnm_g, lnm_b) @ w1 + b1
            slots = jax.nn.gelu(h, approximate=False) @ w2 + b2 + slots
            slots = _ln(slots + x_cls[:, None, :], lnp_g, lnp_b)
        return slots

    def _L0_ffn_ref(x, router_w, expert_w1, expert_w2):
        import jax, jax.numpy as jnp
        import numpy as np
        HIDDEN = 128
        NUM_EXPERTS = 8
        TOP_K = 2
        FFN = 512
        BATCH, SEQ = (4, 256)
        B, S, D = x.shape
        xf = x.reshape(-1, D)
        scores = xf @ router_w.T
        top_v, top_i = jax.lax.top_k(scores, TOP_K)
        routing_w = jax.nn.softmax(top_v, axis=-1)
        out = jnp.zeros_like(xf)
        for e in range(NUM_EXPERTS):
            w_e = jnp.sum(jnp.where(top_i == e, routing_w, 0.0), axis=-1)
            h = jax.nn.gelu(xf @ expert_w1[e].T, approximate=False)
            out = out + h @ expert_w2[e].T * w_e[:, None]
        return out.reshape(B, S, D)

    def _L1_xcond_ref(x, latents, shift, scale, ln1_w, ln1_b, ln2_w, ln2_b, Wq, Wkv, Wo):
        import jax, jax.numpy as jnp
        import numpy as np
        DIM = 128
        DIM_HEAD = 64
        HEADS = 16
        INNER = DIM_HEAD * HEADS
        B, N1, N2 = (8, 512, 32)
        EPS = 1e-05

        def layer_norm(x, w, b):
            mu = jnp.mean(x, axis=-1, keepdims=True)
            var = jnp.var(x, axis=-1, keepdims=True)
            return (x - mu) * jax.lax.rsqrt(var + EPS) * w + b
        x = layer_norm(x, ln1_w, ln1_b)
        lat = layer_norm(latents, ln2_w, ln2_b)
        lat = lat * (1.0 + scale[:, None, :]) + shift[:, None, :]
        b, n2, _ = lat.shape
        q = jnp.einsum('bld,ed->ble', lat, Wq)
        kv_in = jnp.concatenate((x, lat), axis=-2)
        kv = jnp.einsum('bld,ed->ble', kv_in, Wkv)
        k, v = jnp.split(kv, 2, axis=-1)

        def to_heads(t):
            bsz, L, _ = t.shape
            return t.reshape(bsz, L, HEADS, DIM_HEAD).transpose(0, 2, 1, 3)
        q, k, v = (to_heads(q), to_heads(k), to_heads(v))
        attn_scale = 1.0 / np.sqrt(np.sqrt(DIM_HEAD)).astype(np.float32)
        logits = jnp.einsum('bhqd,bhkd->bhqk', q * attn_scale, k * attn_scale)
        w = jax.nn.softmax(logits.astype(jnp.float32), axis=-1).astype(logits.dtype)
        out = jnp.einsum('bhqk,bhkd->bhqd', w, v)
        out = out.transpose(0, 2, 1, 3).reshape(b, n2, INNER)
        return jnp.einsum('ble,de->bld', out, Wo)

    def _L1_ffn_ref(hidden_states, gate_W, gate_b, wi_W, wi_b, wo_W, wo_b, lora_A, lora_B):
        import jax, jax.numpy as jnp
        import numpy as np
        B, S, D, F, E, R = (4, 256, 128, 512, 8, 4)
        x = hidden_states
        logits = jnp.einsum('bsd,ed->bse', x, gate_W) + gate_b
        top1 = jnp.argmax(jax.nn.softmax(logits, axis=-1), axis=-1)
        base = jnp.einsum('bsd,fd->bsf', x, wi_W) + wi_b
        out = jnp.zeros_like(x)
        for i in range(lora_A.shape[0]):
            lora = jnp.einsum('bsr,fr->bsf', jnp.einsum('bsd,rd->bsr', x, lora_A[i]), lora_B[i])
            inter = jax.nn.relu(base + lora)
            expert_out = jnp.einsum('bsf,df->bsd', inter, wo_W) + wo_b
            mask = (top1 == i).astype(x.dtype)[..., None]
            out = out + mask * expert_out
        return out

    def _L2_xcond_ref(x, noise_emb, context, src_mask, ctx_mask, n1_w, n1_b, n2_w, n2_b, n3_w, n3_b, qkv_w, so_w, cq_w, ck_w, cv_w, co_w, f1_w, f1_b, f2_w, f2_b):
        import jax, jax.numpy as jnp
        import numpy as np
        NL, D, H, DFF = (6, 128, 16, 512)
        HD = D // H

        def _rope(x):
            L = x.shape[1]
            half = HD // 2
            inv = 1.0 / 10000.0 ** (jnp.arange(half, dtype=jnp.float32) / half)
            ang = jnp.arange(L, dtype=jnp.float32)[:, None] * inv
            cos = jnp.cos(ang)[None, :, None, :]
            sin = jnp.sin(ang)[None, :, None, :]
            x1, x2 = (x[..., :half], x[..., half:])
            return jnp.concatenate([x1 * cos - x2 * sin, x1 * sin + x2 * cos], axis=-1)

        def _ln(x, eps=1e-05):
            m = jnp.mean(x, axis=-1, keepdims=True)
            v = jnp.var(x, axis=-1, keepdims=True)
            return (x - m) * jax.lax.rsqrt(v + eps)

        def _adaln(x, emb, w, b):
            gb = emb[:, 0, :] @ w.T + b
            g, be = jnp.split(gb, 2, axis=-1)
            return _ln(x) * (1.0 + g[:, None, :]) + be[:, None, :]

        def _attn(q, k, v, mask):
            scores = jnp.einsum('bqhd,bkhd->bhqk', q, k) / np.float32(np.sqrt(HD))
            scores = jnp.where(mask[:, None, None, :], jnp.float32(-jnp.inf), scores)
            w = jax.nn.softmax(scores, axis=-1)
            return jnp.einsum('bhqk,bkhd->bqhd', w, v)
        B, L, _ = x.shape
        LC = context.shape[1]
        for i in range(NL):
            xn = _adaln(x, noise_emb, n1_w[i], n1_b[i])
            qkv = xn @ qkv_w[i].T
            q, k, v = jnp.split(qkv, 3, axis=-1)
            q = _rope(q.reshape(B, L, H, HD))
            k = _rope(k.reshape(B, L, H, HD))
            v = v.reshape(B, L, H, HD)
            a = _attn(q, k, v, src_mask).reshape(B, L, D) @ so_w[i].T
            x = x + a
            xn = _adaln(x, noise_emb, n2_w[i], n2_b[i])
            q = _rope((xn @ cq_w[i].T).reshape(B, L, H, HD))
            k = _rope((context @ ck_w[i].T).reshape(B, LC, H, HD))
            v = (context @ cv_w[i].T).reshape(B, LC, H, HD)
            a = _attn(q, k, v, ctx_mask).reshape(B, L, D) @ co_w[i].T
            x = x + a
            xn = _adaln(x, noise_emb, n3_w[i], n3_b[i])
            h = jax.nn.gelu(xn @ f1_w[i].T + f1_b[i], approximate=False)
            x = x + (h @ f2_w[i].T + f2_b[i])
        return x

    def _L2_ffn_ref(x, w_gate, w_up, w_down):
        import jax, jax.numpy as jnp
        import numpy as np
        BLOCK = 32
        W_BITS = 4
        ACT_BITS = 16

        def act_qdq(x):
            qmax = 2.0 ** (ACT_BITS - 1) - 1.0
            scale = jnp.maximum(jnp.max(jnp.abs(x)) / qmax, 1e-12)
            return jnp.clip(jnp.round(x / scale), -qmax - 1.0, qmax) * scale

        def fixed_qdq_u16(x):
            scale = 1.0 / 65536.0
            return jnp.clip(jnp.round(x / scale), 0.0, 65535.0) * scale

        def lpbq_dequant(w):
            O, I = w.shape
            qmax = 2.0 ** (W_BITS - 1) - 1.0
            wb = w.reshape(O, I // BLOCK, BLOCK)
            s = jnp.maximum(jnp.max(jnp.abs(wb), axis=-1, keepdims=True) / qmax, 1e-12)
            wq = jnp.clip(jnp.round(wb / s), -qmax - 1.0, qmax) * s
            return wq.reshape(O, I)
        x = act_qdq(x)
        up = act_qdq(x @ lpbq_dequant(w_up).T)
        gate = act_qdq(x @ lpbq_dequant(w_gate).T)
        sig = fixed_qdq_u16(jax.nn.sigmoid(gate))
        gate = act_qdq(gate * sig)
        o = act_qdq(gate * up)
        return o @ lpbq_dequant(w_down).T

    def _L3_xcond_ref(x, noise_emb, context, src_mask, ctx_mask, n1_w, n1_b, n2_w, n2_b, n3_w, n3_b, qkv_w, so_w, cq_w, ck_w, cv_w, co_w, f1_w, f1_b, f2_w, f2_b):
        import jax, jax.numpy as jnp
        import numpy as np
        NL, D, H, DFF = (6, 128, 16, 512)
        HD = D // H

        def _rope(x):
            L = x.shape[1]
            half = HD // 2
            inv = 1.0 / 10000.0 ** (jnp.arange(half, dtype=jnp.float32) / half)
            ang = jnp.arange(L, dtype=jnp.float32)[:, None] * inv
            cos = jnp.cos(ang)[None, :, None, :]
            sin = jnp.sin(ang)[None, :, None, :]
            x1, x2 = (x[..., :half], x[..., half:])
            return jnp.concatenate([x1 * cos - x2 * sin, x1 * sin + x2 * cos], axis=-1)

        def _ln(x, eps=1e-05):
            m = jnp.mean(x, axis=-1, keepdims=True)
            v = jnp.var(x, axis=-1, keepdims=True)
            return (x - m) * jax.lax.rsqrt(v + eps)

        def _adaln(x, emb, w, b):
            gb = emb[:, 0, :] @ w.T + b
            g, be = jnp.split(gb, 2, axis=-1)
            return _ln(x) * (1.0 + g[:, None, :]) + be[:, None, :]

        def _attn(q, k, v, mask):
            scores = jnp.einsum('bqhd,bkhd->bhqk', q, k) / np.float32(np.sqrt(HD))
            scores = jnp.where(mask[:, None, None, :], jnp.float32(-jnp.inf), scores)
            w = jax.nn.softmax(scores, axis=-1)
            return jnp.einsum('bhqk,bkhd->bqhd', w, v)
        B, L, _ = x.shape
        LC = context.shape[1]
        for i in range(NL):
            xn = _adaln(x, noise_emb, n1_w[i], n1_b[i])
            qkv = xn @ qkv_w[i].T
            q, k, v = jnp.split(qkv, 3, axis=-1)
            q = _rope(q.reshape(B, L, H, HD))
            k = _rope(k.reshape(B, L, H, HD))
            v = v.reshape(B, L, H, HD)
            a = _attn(q, k, v, src_mask).reshape(B, L, D) @ so_w[i].T
            x = x + a
            xn = _adaln(x, noise_emb, n2_w[i], n2_b[i])
            q = _rope((xn @ cq_w[i].T).reshape(B, L, H, HD))
            k = _rope((context @ ck_w[i].T).reshape(B, LC, H, HD))
            v = (context @ cv_w[i].T).reshape(B, LC, H, HD)
            a = _attn(q, k, v, ctx_mask).reshape(B, L, D) @ co_w[i].T
            x = x + a
            xn = _adaln(x, noise_emb, n3_w[i], n3_b[i])
            h = jax.nn.gelu(xn @ f1_w[i].T + f1_b[i], approximate=False)
            x = x + (h @ f2_w[i].T + f2_b[i])
        return x

    def _L3_ffn_ref(x, gate_query, log_temp, w1, b1, w2, b2):
        import jax, jax.numpy as jnp
        import numpy as np
        B, N, D, E, DFF = (4, 256, 128, 16, 512)
        CAPACITY_FACTOR = 2.0
        CAP = int(N * CAPACITY_FACTOR / E)
        SINKHORN_ITERS = 6

        def _sinkhorn(logits, n_iters=SINKHORN_ITERS, tau=1.0):
            t = logits / tau
            for _ in range(n_iters):
                t = t - jax.scipy.special.logsumexp(t, axis=-2, keepdims=True)
                t = t - jax.scipy.special.logsumexp(t, axis=-1, keepdims=True)
            return jnp.exp(t)
        b, n, d = x.shape
        gate_logits = jnp.einsum('bnd,ed->ben', x, gate_query)
        affinity_logits = gate_logits / jnp.exp(log_temp)
        affinity = _sinkhorn(affinity_logits)
        gates, idx = jax.lax.top_k(affinity, CAP)
        expert_in = jnp.take_along_axis(x[:, None, :, :], idx[..., None], axis=2)
        h = jax.nn.gelu(jnp.einsum('becd,edf->becf', expert_in, w1) + b1[None, :, None, :])
        expert_out = jnp.einsum('becf,efd->becd', h, w2) + b2[None, :, None, :]
        out = jnp.zeros_like(x)
        out = out.at[jnp.arange(b)[:, None, None], idx].add(gates[..., None] * expert_out)
        return out
    x = x + _L0_xcond_ref(cond_1024, ctx_1024, _layernorm(x, axis=-1), L0_xcond_q_mu, L0_xcond_q_logsig, L0_xcond_lnkv_g, L0_xcond_lnkv_b, L0_xcond_lnq_g, L0_xcond_lnq_b, L0_xcond_lnm_g, L0_xcond_lnm_b, L0_xcond_lnp_g, L0_xcond_lnp_b, L0_xcond_wk, L0_xcond_bk, L0_xcond_wv, L0_xcond_bv, L0_xcond_wq, L0_xcond_bq, L0_xcond_wu, L0_xcond_bu, L0_xcond_w1, L0_xcond_b1, L0_xcond_w2, L0_xcond_b2)
    x = x + _L0_ffn_ref(_layernorm(x, axis=-1), L0_ffn_router_w, L0_ffn_expert_w1, L0_ffn_expert_w2)
    x = x + _L1_xcond_ref(ctx_1024, _layernorm(x, axis=-1), cond_1024, cond_1024, L1_xcond_ln1_w, L1_xcond_ln1_b, L1_xcond_ln2_w, L1_xcond_ln2_b, L1_xcond_Wq, L1_xcond_Wkv, L1_xcond_Wo)
    x = x + _L1_ffn_ref(_layernorm(x, axis=-1), L1_ffn_gate_W, L1_ffn_gate_b, L1_ffn_wi_W, L1_ffn_wi_b, L1_ffn_wo_W, L1_ffn_wo_b, L1_ffn_lora_A, L1_ffn_lora_B)
    x = x + _L2_xcond_ref(_layernorm(x, axis=-1), cond_1024[:, None, :], ctx_1024, mask_BxS_bf0, mask_BxS2_bf0, L2_xcond_n1_w, L2_xcond_n1_b, L2_xcond_n2_w, L2_xcond_n2_b, L2_xcond_n3_w, L2_xcond_n3_b, L2_xcond_qkv_w, L2_xcond_so_w, L2_xcond_cq_w, L2_xcond_ck_w, L2_xcond_cv_w, L2_xcond_co_w, L2_xcond_f1_w, L2_xcond_f1_b, L2_xcond_f2_w, L2_xcond_f2_b)
    x = x + _L2_ffn_ref(_layernorm(x, axis=-1), L2_ffn_w_gate, L2_ffn_w_up, L2_ffn_w_down)
    x = x + _L3_xcond_ref(_layernorm(x, axis=-1), cond_1024[:, None, :], ctx_1024, mask_BxS_bf0, mask_BxS2_bf0, L3_xcond_n1_w, L3_xcond_n1_b, L3_xcond_n2_w, L3_xcond_n2_b, L3_xcond_n3_w, L3_xcond_n3_b, L3_xcond_qkv_w, L3_xcond_so_w, L3_xcond_cq_w, L3_xcond_ck_w, L3_xcond_cv_w, L3_xcond_co_w, L3_xcond_f1_w, L3_xcond_f1_b, L3_xcond_f2_w, L3_xcond_f2_b)
    x = x + _L3_ffn_ref(_layernorm(x, axis=-1), L3_ffn_gate_query, L3_ffn_log_temp, L3_ffn_w1, L3_ffn_b1, L3_ffn_w2, L3_ffn_b2)
    return x

_drawn_inputs = setup_inputs


def setup_inputs(seed=0):
    import zlib

    import numpy as np

    out = dict(_drawn_inputs(seed))
    spreads = {'L0_xcond_lnkv_g': (1.0, 0.6),
     'L0_xcond_lnkv_b': (0.0, 0.8),
     'L0_xcond_lnq_g': (1.0, 0.6),
     'L0_xcond_lnq_b': (0.0, 2.0),
     'L0_xcond_lnm_g': (1.0, 0.6),
     'L0_xcond_lnm_b': (0.0, 0.8),
     'L0_xcond_lnp_g': (1.0, 0.2),
     'L0_xcond_lnp_b': (0.0, 0.1),
     'L0_xcond_bk': (0.0, 0.618),
     'L0_xcond_bv': (0.0, 0.308),
     'L0_xcond_bq': (0.0, 2.0),
     'L0_xcond_bu': (0.0, 0.1),
     'L0_xcond_b1': (0.0, 0.493),
     'L0_xcond_b2': (0.0, 0.1),
     'L1_xcond_ln1_w': (1.0, 0.6),
     'L1_xcond_ln1_b': (0.0, 0.8),
     'L1_xcond_ln2_w': (1.0, 0.6),
     'L1_xcond_ln2_b': (0.0, 0.8),
     'L1_ffn_gate_b': (0.0, 0.8),
     'L1_ffn_wi_b': (0.0, 0.1),
     'L1_ffn_wo_b': (0.0, 0.1),
     'L2_xcond_n1_b': (0.0, 0.8),
     'L2_xcond_n2_b': (0.0, 0.8),
     'L2_xcond_n3_b': (0.0, 0.8),
     'L2_xcond_f1_b': (0.0, 0.367),
     'L2_xcond_f2_b': (0.0, 0.1),
     'L3_xcond_n1_b': (0.0, 0.8),
     'L3_xcond_n2_b': (0.0, 0.8),
     'L3_xcond_n3_b': (0.0, 0.8),
     'L3_xcond_f1_b': (0.0, 0.528),
     'L3_xcond_f2_b': (0.0, 0.1),
     'L3_ffn_b1': (0.0, 2.0),
     'L3_ffn_b2': (0.0, 2.0)}
    factors = {'L0_xcond_q_logsig': 4.267,
     'L1_xcond_Wq': 7.358,
     'L1_ffn_gate_W': 3.311,
     'L1_ffn_lora_A': 3.396,
     'L1_ffn_lora_B': 3.242,
     'L2_xcond_n1_w': 4.65,
     'L2_xcond_n2_w': 8.0,
     'L2_xcond_n3_w': 3.842,
     'L2_xcond_cq_w': 8.0,
     'L2_xcond_ck_w': 8.0,
     'L2_ffn_w_gate': 8.0,
     'L2_ffn_w_up': 8.0,
     'L2_ffn_w_down': 8.0,
     'L3_xcond_n1_w': 6.363,
     'L3_xcond_n2_w': 8.0,
     'L3_xcond_n3_w': 5.272,
     'L3_xcond_cq_w': 8.0,
     'L3_xcond_ck_w': 8.0,
     'L3_xcond_cv_w': 3.212,
     'L3_xcond_co_w': 3.302,
     'L3_ffn_gate_query': 8.0,
     'L3_ffn_w1': 8.0,
     'L3_ffn_w2': 8.0}
    for name, (base, spread) in spreads.items():
        noise = np.random.default_rng([zlib.crc32(name.encode()), seed]).standard_normal(out[name].shape)
        drawn = base * np.exp(spread * noise) if base else spread * noise
        out[name] = jnp.asarray(drawn.astype(out[name].dtype))
    for name, factor in factors.items():
        out[name] = (out[name] * factor).astype(out[name].dtype)
    return out
```

```python
from contextlib import ExitStack

import numpy as np

import concourse.bass as bass
from concourse import mybir
from concourse.alu_op_type import AluOpType as ALU

F32 = mybir.dt.float32
BF16 = mybir.dt.bfloat16
U8 = mybir.dt.uint8
ACT = mybir.ActivationFunctionType
AX = mybir.AxisListType

FIRST, LAST = 0, 7

P = 128
D = 128
B, S = 2, 512
T = B * S
CTX = 154
NL = 6
H, HD = 16, 8
DFF = 512
FT = DFF // P
MASK_BYTES = -(-(S + CTX) // 4) * 4
GROUPS = 4
HG = H // GROUPS
BG = B * GROUPS
KS, KC = S // P, 2
CP = KC * P
EPS = 1e-5
NEG = -3.0e38

W_NORM, W_SELF, W_CROSS, W_SOUT, W_COUT, W_F1, W_F2 = 0, 768, 1408, 2048, 2560, 3072, 3584
W_ALL = 4096
SECTIONS = [(W_NORM, W_SELF), (W_SELF, W_CROSS), (W_CROSS, W_SOUT), (W_SOUT, W_COUT), (W_COUT, W_F1), (W_F1, W_ALL)]
SEC_NORM, SEC_SELF, SEC_CROSS, SEC_SOUT, SEC_COUT, SEC_FFN = range(6)
NBIAS = 11

PARTS = 6
ROW_MASK = PARTS * HD
ROW_MAX = ROW_MASK + 1
K_SCORE = ROW_MASK + 1
K_EXP = ROW_MAX + 3
Q_SLOTS = [0, 1, 2, 0, 1, 0]
K_SLOTS = [0, 0, 0, 1, 1, 2]


def ring_order(kt):
    out = [("max", 0, 0)]
    for g in range(BG):
        for s in range(2 * kt):
            if s == kt and g + 1 < BG:
                out.append(("max", g + 1, 0))
            out.append(("exp", g, s))
    return out


RING_SELF, RING_CROSS = ring_order(KS), ring_order(KC)
RING_LAYER = len(RING_SELF) + len(RING_CROSS)


def build(nc, dram):
    with ExitStack() as ctx:
        def sb(name, shape, dt=F32):
            return ctx.enter_context(nc.sbuf_tensor(name, shape, dt))

        def sem(name):
            return ctx.enter_context(nc.semaphore(name))

        ps = ctx.enter_context(nc.psum_tensor("ps", [P, 8 * 512], F32))

        def bank(k, n=1):
            return ps[:, 512 * k:512 * (k + n)]

        x = sb("x", [P, T])
        h = sb("h", [P, T])
        xn = sb("xn", [P, T])
        sq = sb("sq", [P, T])
        lg = sb("lg", [P, T])
        rstd = sb("rstd", [P, T])
        tmp = sb("tmp", [P, T])
        consts = sb("consts", [P, 4 * P])
        center, mean_w, selector, ident = (consts[:, P * i:P * (i + 1)] for i in range(4))
        identb = sb("identb", [P, P], BF16)
        rope = sb("rope", [P, 2, S])
        ctxT = sb("ctxT", [P, B * CTX])
        condT = sb("condT", [P, B])
        epst = sb("epst", [P, 1])
        zeros = sb("zeros", [P, 16])

        w = sb("w", [P, W_ALL])
        bias_all = sb("bias_all", [P, 2 * NL * NBIAS])
        bias = sb("bias", [P, NBIAS])

        ARENA = 36352
        arena = sb("arena", [P, ARENA])
        used = [0]

        def carve(cols, dt=F32):
            a = arena[:, used[0]:used[0] + cols]
            used[0] += -(-cols // 8) * 8
            assert used[0] <= ARENA, used[0]
            return a if dt == F32 else a.bitcast(dt)

        gains = carve(12).rearrange("p (k w b) -> p k w b", k=3, w=2)
        parts = carve(4 * 3 * S // 2, BF16).rearrange("p (u c n) -> p u c n", u=4, c=3)
        parts_c = carve(3 * B * CTX // 2, BF16).rearrange("p (c n) -> p c n", c=3)
        qst = carve(H * S // 2, BF16).rearrange("p (h n) -> p h n", h=H)
        kst = carve(H * S // 2, BF16).rearrange("p (h n) -> p h n", h=H)
        kstc = carve(H * CP // 2, BF16).rearrange("p (h n) -> p h n", h=H)
        vaug = carve(B * KS * H * 32).rearrange("p (b k h c) -> p b k h c", b=B, k=KS, h=H)
        vaugc = carve(B * KC * H * 32).rearrange("p (b k h c) -> p b k h c", b=B, k=KC, h=H)
        prob = carve(3 * HG * S).rearrange("p (r j n) -> p r j n", r=3, j=HG)
        hid = prob.rearrange("p r j n -> p (r j n)")[:, 0:FT * T].rearrange("p (t n) -> p t n", t=FT)
        att = carve(BG * S).rearrange("p (g n) -> p g n", g=BG)
        osb = carve(2 * S).rearrange("p (g n) -> p g n", g=2)
        rlog = carve(S)
        rinv = carve(2 * S).rearrange("p (g n) -> p g n", g=2)
        nmax = carve(32).rearrange("p (g c) -> p g c", g=2)
        nrem = carve(32).rearrange("p (g c) -> p g c", g=2)
        nmaxp = carve(48, BF16).rearrange("p (g c) -> p g c", g=2)
        nmaxT = carve(P, BF16).rearrange("p (g c) -> p g c", g=2)

        loaded = sem("loaded")
        x_loaded = sem("x_loaded")
        x_ready = sem("x_ready")
        ln_centered, ln_squared, ln_variance = sem("ln_centered"), sem("ln_squared"), sem("ln_variance")
        ln_logged, ln_rstd, ln_scaled, ln_done = sem("ln_logged"), sem("ln_rstd"), sem("ln_scaled"), sem("ln_done")
        setup_done = sem("setup_done")
        const_rows = sem("const_rows")
        bias_loaded = sem("bias_loaded")
        w_loaded = [sem(f"w_loaded{i}") for i in range(len(SECTIONS))]
        bias_copied, gain_mm, gains_ready = sem("bias_copied"), sem("gain_mm"), sem("gains_ready")
        proj_mm = sem("proj_mm")
        rope_mul, rope_sum = sem("rope_mul"), sem("rope_sum")
        part_hi, part_rem, part_mid, part_lo = sem("part_hi"), sem("part_rem"), sem("part_mid"), sem("part_lo")
        stacked_q = [sem(f"stacked_q{b}") for b in range(B)]
        stacked_k = [sem(f"stacked_k{b}") for b in range(B)]
        stacked_c = sem("stacked_c")
        v_mm, v_copied = sem("v_mm"), sem("v_copied")
        score_mm, score_max = sem("score_mm"), sem("score_max")
        max_split = sem("max_split")
        ring_mm, ring_read = sem("ring_mm"), sem("ring_read")
        max_row = [sem(f"max_row{i}") for i in range(2)]
        pv_mm, o_copied = sem("pv_mm"), sem("o_copied")
        den_mm, den_log, den_inv, att_ready = sem("den_mm"), sem("den_log"), sem("den_inv"), sem("att_ready")
        out_mm = sem("out_mm")
        h_ready = sem("h_ready")
        hid_mm, hid_ready = sem("hid_mm"), sem("hid_ready")
        stored = sem("stored")

        def cols(a, b, width=S):
            return a[:, b * width:(b + 1) * width]

        def ln_pe(pe, n, src, ready, width=S):
            for b in range(B):
                ready(pe, b)
                pe.matmul(bank(b)[:, 0:width], center, cols(src, b, width), start=True, stop=True)\
                  .then_inc(ln_centered, 1)
            for b in range(B):
                pe.wait_ge(ln_squared, 2 * n + b + 1)
                pe.matmul(bank(2 + b)[:, 0:width], mean_w, cols(sq, b)[:, 0:width], start=True, stop=True)\
                  .then_inc(ln_variance, 1)

        def both_log_and_exp(act):
            act.preload_act_table_set("natural_log_exp_and_others")

        def ln_act(act, n, width=S):
            for b in range(B):
                act.wait_ge(ln_centered, 2 * n + b + 1)
                act.activation(cols(sq, b)[:, 0:width], bank(b)[:, 0:width], ACT.Square).then_inc(ln_squared, 1)
            for b in range(B):
                act.wait_ge(ln_variance, 2 * n + b + 1)
                act.activation(cols(lg, b)[:, 0:width], bank(2 + b)[:, 0:width], ACT.Ln, bias=epst[:, 0:1])\
                   .then_inc(ln_logged, 1)
                act.wait_ge(ln_logged, 2 * n + b + 1)
                act.activation(cols(rstd, b)[:, 0:width], cols(lg, b)[:, 0:width], ACT.Exp, scale=-0.5)\
                   .then_inc(ln_rstd, 1)

        def ln_dve(ve, n, dst, gain=None, shift=None, width=S, scaled=0, done=None):
            for b in range(B):
                ve.wait_ge(ln_rstd, 2 * n + b + 1)
                c, r = bank(b)[:, 0:width], cols(rstd, b)[:, 0:width]
                d = dst(b) if callable(dst) else cols(dst, b, width)
                if gain is None:
                    ve.tensor_tensor(d, c, r, ALU.mult).then_inc(done or ln_done, 1)
                    continue
                t = cols(tmp, b)[:, 0:width]
                ve.scalar_tensor_tensor(t, c, gain(b), r, ALU.mult, ALU.mult).then_inc(ln_scaled, 1)
                ve.wait_ge(ln_scaled, 2 * scaled + b + 1)
                ve.tensor_scalar(d, t, shift(b), None, ALU.add).then_inc(done or ln_done, 1)

        def unit_width(u):
            return B * CTX if u == 4 else S

        UNIT_BANKS = [4, 6, 0, 2, 2, 4, 6]
        def unit_parts(u):
            if u == 4:
                return parts_c
            return parts[:, u if u < 4 else 2 * (u - 5)]

        def unit_half(a, u):
            return cols(a, u % 2)[:, 0:unit_width(u)]

        def pe_unit(pe, l, u):
            wq = w[:, {0: W_SELF, 1: W_SELF + 256, 2: W_SELF, 3: W_SELF + 256, 4: W_CROSS + 256, 5: W_CROSS, 6: W_CROSS}[u]:]
            src = ctxT[:, :] if u == 4 else cols(xn, {0: 0, 1: 0, 2: 1, 3: 1, 5: 0, 6: 1}[u])
            for i in range(2):
                mm = pe.matmul(bank(UNIT_BANKS[u] + i)[:, 0:unit_width(u)], wq[:, P * i:P * (i + 1)], src,
                               start=True, stop=True)
            mm.then_inc(proj_mm, 1)

        def dve_unit(ve, l, u):
            n = unit_width(u)
            ve.wait_ge(proj_mm, 7 * l + u + 1)
            if u >= 2 and u != 5:
                ve.wait_ge(part_lo, 7 * l + u - 1)
            for i, dst in enumerate((sq, lg)):
                if u == 4:
                    for b in range(B):
                        mul = ve.tensor_tensor(unit_half(dst, u)[:, b * CTX:(b + 1) * CTX],
                                               bank(UNIT_BANKS[u] + i)[:, b * CTX:(b + 1) * CTX],
                                               rope[:, i, 0:CTX], ALU.mult)
                        mul.then_inc(rope_mul, 1) if b == 1 else None
                else:
                    ve.tensor_tensor(unit_half(dst, u), bank(UNIT_BANKS[u] + i)[:, 0:n], rope[:, i, 0:n], ALU.mult)\
                      .then_inc(rope_mul, 1)
            ve.wait_ge(rope_mul, 14 * l + 2 * u + 2)
            ve.tensor_tensor(unit_half(rstd, u), unit_half(sq, u), unit_half(lg, u), ALU.add).then_inc(rope_sum, 1)

        def act_unit(act, l, u, step):
            p = unit_parts(u)
            if step == 0:
                act.wait_ge(rope_sum, 7 * l + u + 1)
                act.activation(p[:, 0], unit_half(rstd, u), ACT.Copy).then_inc(part_hi, 1)
            else:
                act.wait_ge(part_rem, 7 * l + u + 1)
                act.activation(p[:, 1], unit_half(tmp, u), ACT.Copy).then_inc(part_mid, 1)

        def pool_unit(gp, l, u):
            p = unit_parts(u)
            gp.wait_ge(part_hi, 7 * l + u + 1)
            gp.tensor_tensor(unit_half(tmp, u), unit_half(rstd, u), p[:, 0], ALU.subtract).then_inc(part_rem, 1)
            gp.wait_ge(part_mid, 7 * l + u + 1)
            gp.tensor_tensor(p[:, 2], unit_half(tmp, u), p[:, 1], ALU.subtract).then_inc(part_lo, 1)

        def sp_unit(sp, l, u):
            key = u in (1, 3, 4)
            slots = K_SLOTS if key else Q_SLOTS
            dst = kstc if u == 4 else kst if key else qst
            p = unit_parts(u)
            for part, ready in enumerate((part_hi, part_mid, part_lo)):
                sp.wait_ge(ready, 7 * l + u + 1)
                for slot in range(PARTS):
                    if slots[slot] != part:
                        continue
                    for b in ((0, 1) if u == 4 else ({0: 0, 1: 0, 2: 1, 3: 1, 5: 0, 6: 1}[u],)):
                        row = 64 * b + HD * slot
                        src = p[:, part, b * CTX:(b + 1) * CTX] if u == 4 else p[:, part, :]
                        n = CTX if u == 4 else S
                        done = stacked_c if u == 4 else (stacked_k if key else stacked_q)[b]
                        sp.dma_start(dst[row:row + HD, :, 0:n], src).then_inc(done, 16)

        class Attention:
            def __init__(self, l, a):
                self.a, self.kt = a, (KS, KC)[a]
                self.order = (RING_SELF, RING_CROSS)[a]
                self.k = (kst, kstc)[a]
                self.v = (vaug, vaugc)[a]
                self.nkeys = (S, CTX)[a]
                self.tile0 = l * (2 * 128) + 128 * a
                self.ring0 = l * RING_LAYER + len(RING_SELF) * a
                self.chunk0 = l * (BG * (KS + KC)) + BG * KS * a
                self.group0 = l * (2 * BG) + BG * a
                self.chunk_local0 = BG * KS * a
                self.sc = (W_SOUT, W_COUT)[a]

        def ring_slot(e):
            return bank(2 + 2 * (e % 2), 2)

        def head(g, j):
            return g // GROUPS, (g % GROUPS) * HG + j

        def pe_attention(pe, l, a):
            t = Attention(l, a)
            kt_n = t.kt

            def score(i):
                g, j, qt = i // 16, i % 16 // 4, i % 4
                b, hd = head(g, j)
                if i % 64 == 0:
                    pe.wait_ge(stacked_q[b], 16 * PARTS * (2 * l + a + 1))
                    if a == 0:
                        pe.wait_ge(stacked_k[b], 16 * PARTS * (l + 1))
                    elif b == 0:
                        pe.wait_ge(stacked_c, 32 * PARTS * (l + 1))
                if i >= 2 or a == 1:
                    pe.wait_ge(score_max, t.tile0 + i - 1)
                r = 64 * b
                pe.matmul(bank(i % 2)[:, 0:t.nkeys], qst[r:r + K_SCORE, hd, qt * P:(qt + 1) * P],
                          t.k[r:r + K_SCORE, hd, 0:t.nkeys], start=True, stop=True).then_inc(score_mm, 1)

            def ring_free(e):
                if e >= 2 or a == 1:
                    pe.wait_ge(ring_read, t.ring0 + e - 1)

            def turn_max(e, g):
                pe.wait_ge(max_split, 4 * (t.group0 + g + 1))
                ring_free(e)
                pe.matmul(ring_slot(e)[0:48, 0:P], nmaxp[:, g % 2, :], identb[:, :], start=True, stop=True)\
                  .then_inc(ring_mm, 1)

            def exp_scores(e, g, s):
                kt, pr = s // 2, s % 2
                if s == 0:
                    pe.wait_ge(max_row[g % 2], 16 * (l * BG + a * (BG // 2) + g // 2 + 1))
                ring_free(e)
                for jj in range(2):
                    b, hd = head(g, 2 * pr + jj)
                    r = 64 * b
                    mm = pe.matmul(ring_slot(e)[:, jj * S:(jj + 1) * S], t.k[r:r + K_EXP, hd, kt * P:(kt + 1) * P],
                                   qst[r:r + K_EXP, hd, :], start=True, stop=True)
                mm.then_inc(ring_mm, 1)

            def weigh_values(g, kt):
                if g == 0 and kt == 0:
                    pe.wait_ge(v_copied, 6 * l + (4 if a == 0 else 6))
                if kt == 0 and g >= 2:
                    pe.wait_ge(den_log, t.group0 + g - 1)
                e = t.order.index(("exp", g, 2 * kt + 1))
                pe.wait_ge(ring_read, t.ring0 + e + 1)
                slot = (t.chunk_local0 + g * kt_n + kt) % 3
                for j in range(HG):
                    b, hd = head(g, j)
                    mm = pe.matmul(bank(6 + g % 2)[32 * j:32 * j + 32, :], t.v[:, b, kt, hd, :], prob[:, slot, j, :],
                                   start=(kt == 0), stop=(kt == kt_n - 1))
                mm.then_inc(pv_mm, 1)

            def denominators(g):
                pe.wait_ge(o_copied, t.group0 + g + 1)
                pe.matmul(bank(6 + g % 2), selector, osb[:, g % 2, :], start=True, stop=True).then_inc(den_mm, 1)

            for i in range(24):
                score(i)
            turn_max(0, 0)
            for i in range(24, 32):
                score(i)
            i = 32
            for e, (kind, g, s) in enumerate(t.order):
                if e == 0:
                    continue
                if kind == "max":
                    turn_max(e, g)
                    continue
                exp_scores(e, g, s)
                for _ in range(16 // (2 * kt_n)):
                    if i < 128:
                        score(i)
                        i += 1
                if s == 1 and g > 0:
                    weigh_values(g - 1, kt_n - 1)
                if s % 2 == 1 and s >= 3:
                    weigh_values(g, (s - 3) // 2)
                if s == 2 * kt_n - 1 and g > 0:
                    denominators(g - 1)
            weigh_values(BG - 1, kt_n - 1)
            denominators(BG - 1)
            sec = (SEC_SOUT, SEC_COUT)[a]
            for b in range(B):
                pe.wait_ge(att_ready, t.group0 + GROUPS * (b + 1))
                pe.wait_ge(den_log, t.group0 + BG - 1 + b)
                if b == 0:
                    pe.wait_ge(w_loaded[sec], 16 * (l + 1))
                for g in range(GROUPS):
                    mm = pe.matmul(bank(6 + b), w[:, t.sc + P * g:t.sc + P * (g + 1)], att[:, GROUPS * b + g, :],
                                   start=(g == 0), stop=(g == GROUPS - 1))
                mm.then_inc(out_mm, 1)

        def act_attention(act, l, a):
            t = Attention(l, a)

            def copy_out(g):
                act.wait_ge(pv_mm, t.chunk0 + (g + 1) * t.kt)
                if g >= 2:
                    act.wait_ge(att_ready, t.group0 + g - 1)
                act.activation(osb[:, g % 2, :], bank(6 + g % 2), ACT.Copy).then_inc(o_copied, 1)

            def invert(g):
                act.wait_ge(den_mm, t.group0 + g + 1)
                if g >= 1:
                    act.wait_ge(den_inv, t.group0 + g)
                act.activation(rlog, bank(6 + g % 2), ACT.Ln).then_inc(den_log, 1)
                act.wait_ge(den_log, t.group0 + g + 1)
                if g >= 2:
                    act.wait_ge(att_ready, t.group0 + g - 1)
                act.activation(rinv[:, g % 2, :], rlog, ACT.Exp, scale=-1.0).then_inc(den_inv, 1)

            for e, (kind, g, s) in enumerate(t.order):
                act.wait_ge(ring_mm, t.ring0 + e + 1)
                if kind == "max":
                    if g >= 2:
                        act.wait_ge(max_row[g % 2], 16 * (l * BG + a * (BG // 2) + g // 2))
                    act.activation(nmaxT[0:48, g % 2, :], ring_slot(e)[0:48, 0:P], ACT.Copy)\
                       .then_inc(ring_read, 1)
                    continue
                kt, pr = s // 2, s % 2
                chunk = g * t.kt + kt
                if chunk >= 3 or a == 1:
                    act.wait_ge(pv_mm, t.chunk0 + chunk - 2)
                slot = (t.chunk_local0 + chunk) % 3
                act.activation(prob[:, slot, 2 * pr:2 * pr + 2, :], ring_slot(e).rearrange("p (j n) -> p j n", j=2),
                               ACT.Exp, scale=float(HD) ** -0.5).then_inc(ring_read, 1)
                if s == 1 and g >= 2:
                    invert(g - 2)
                if s == 2 and g >= 1:
                    copy_out(g - 1)
            invert(BG - 2)
            copy_out(BG - 1)
            invert(BG - 1)

        def pool_attention(gp, l, a):
            t = Attention(l, a)

            def split_max(g):
                n, at = g % 2, 4 * (t.group0 + g)
                hi, mid, lo = (nmaxp[:, n, 16 * i:16 * (i + 1)] for i in range(3))
                gp.wait_ge(score_max, t.tile0 + 16 * (g + 1))
                if g >= 2:
                    gp.wait_ge(ring_mm, t.ring0 + t.order.index(("max", g - 2, 0)) + 1)
                gp.tensor_tensor(hi, nmax[:, n, :], zeros[:, :], ALU.add).then_inc(max_split, 1)
                gp.wait_ge(max_split, at + 1)
                gp.tensor_tensor(nrem[:, n, :], nmax[:, n, :], hi, ALU.subtract).then_inc(max_split, 1)
                gp.wait_ge(max_split, at + 2)
                gp.tensor_tensor(mid, nrem[:, n, :], zeros[:, :], ALU.add).then_inc(max_split, 1)
                gp.wait_ge(max_split, at + 3)
                gp.tensor_tensor(lo, nrem[:, n, :], mid, ALU.subtract).then_inc(max_split, 1)

            def normalise(g):
                gp.wait_ge(den_inv, t.group0 + g + 1)
                gp.tensor_tensor(att[:, g, :], osb[:, g % 2, :], rinv[:, g % 2, :], ALU.mult).then_inc(att_ready, 1)

            split_max(0)
            split_max(1)
            for g in range(BG):
                if g >= 2:
                    normalise(g - 2)
                if g + 2 < BG:
                    split_max(g + 2)
            normalise(BG - 2)
            normalise(BG - 1)

        def dve_attention(ve, l, a, c):
            t = Attention(l, a)
            for i in range(128):
                g = i // 16
                ve.wait_ge(score_mm, t.tile0 + i + 1)
                if i % 16 == 0 and (g >= 2 or a == 1):
                    ve.wait_ge(max_split, 4 * (t.group0 + g - 1))
                ve.tensor_reduce(nmax[:, g % 2, i % 16:i % 16 + 1], bank(i % 2)[:, 0:t.nkeys], AX.X, ALU.max,
                                 negate=True).then_inc(score_max, 1)
            for b in range(B):
                ve.wait_ge(out_mm, 6 * l + 2 * a + b + 1)
                ve.tensor_tensor(cols(h, b), bank(6 + b), cols(h, b), ALU.add).then_inc(h_ready, 1)

        def sp_attention(sp, l, a):
            t = Attention(l, a)
            for g in range(BG):
                e = t.order.index(("max", g, 0))
                b = g // GROUPS
                h0 = (g % GROUPS) * HG
                sp.wait_ge(ring_read, t.ring0 + e + 1)
                sp.dma_start(qst[64 * b + ROW_MAX:64 * b + ROW_MAX + 3, h0:h0 + HG, :], nmaxT[0:48, g % 2, :])\
                  .then_inc(max_row[g % 2], 16)

        def h_is(l, k, c):
            return lambda eng, b: eng.wait_ge(h_ready, c["h"] + 6 * l + 2 * k - 2 + b + 1)

        def pe_layer(pe, l, c):
            def norm(k):
                ln_pe(pe, c["ln"] + 3 * l + k, h, h_is(l, k, c))
                return 2 * (c["done"] + 3 * l + k)

            pe.wait_ge(w_loaded[SEC_NORM], 16 * (l + 1))
            for k in range(6):
                mm = pe.matmul(bank(4)[:, 2 * k:2 * k + 2], w[:, W_NORM + P * k:W_NORM + P * (k + 1)], condT[:, :],
                               start=True, stop=True)
            mm.then_inc(gain_mm, 1)
            n = norm(0)
            pe.wait_ge(w_loaded[SEC_SELF], 16 * (l + 1))
            pe.wait_ge(gains_ready, 4 * (l + 1))
            for u in range(4):
                if u % 2 == 0:
                    pe.wait_ge(ln_done, n + u // 2 + 1)
                pe_unit(pe, l, u)
            for b in range(B):
                pe.wait_ge(rope_mul, 14 * l + 2 * b + 2)
                for t in range(KS):
                    mm = pe.matmul(bank(4 + 2 * b)[:, P * t:P * (t + 1)], xn[:, b * S + P * t:b * S + P * (t + 1)],
                                   w[:, W_SELF + 512:W_SELF + 640], start=True, stop=True)
                mm.then_inc(v_mm, 1)
            pe.wait_ge(w_loaded[SEC_CROSS], 16 * (l + 1))
            for b in range(B):
                pe.matmul(bank(5)[:, 256 * b:256 * b + P], ctxT[:, b * CTX:b * CTX + P],
                          w[:, W_CROSS + 512:W_CROSS + 640], start=True, stop=True)
                mm = pe.matmul(bank(5)[0:CTX - P, 256 * b + P:256 * b + 2 * P], ctxT[:, b * CTX + P:(b + 1) * CTX],
                               w[:, W_CROSS + 512:W_CROSS + 640], start=True, stop=True)
            mm.then_inc(v_mm, 1)
            pe.wait_ge(rope_mul, 14 * l + 8)
            pe_unit(pe, l, 4)
            pe_attention(pe, l, 0)

            n = norm(1)
            for u in (5, 6):
                pe.wait_ge(ln_done, n + u - 4)
                pe_unit(pe, l, u)
            pe_attention(pe, l, 1)

            n = norm(2)
            pe.wait_ge(w_loaded[SEC_FFN], 16 * (l + 1))
            for f in range(B * FT):
                b, t = f // FT, f % FT
                if t == 0:
                    pe.wait_ge(ln_done, n + b + 1)
                if f >= 4:
                    pe.wait_ge(hid_ready, B * FT * l + f - 3)
                pe.matmul(bank(4 + f % 4), w[:, W_F1 + P * t:W_F1 + P * (t + 1)], cols(xn, b), start=True, stop=True)\
                  .then_inc(hid_mm, 1)
            for b in range(B):
                pe.wait_ge(hid_ready, B * FT * l + FT * (b + 1))
                for t in range(FT):
                    mm = pe.matmul(bank(b), w[:, W_F2 + P * t:W_F2 + P * (t + 1)], hid[:, t, b * S:(b + 1) * S],
                                   start=(t == 0), stop=(t == FT - 1))
                mm.then_inc(out_mm, 1)

        def act_layer(act, l, c):
            both_log_and_exp(act)
            ln_act(act, c["ln"] + 3 * l)
            act_unit(act, l, 0, 0)
            for u in range(1, 4):
                act_unit(act, l, u, 0)
                act_unit(act, l, u - 1, 1)
            act_unit(act, l, 3, 1)
            for b in range(B):
                act.wait_ge(v_mm, 3 * l + b + 1)
                for t in range(KS):
                    cp = act.activation(vaug[:, b, t, :, 0:HD],
                                        bank(4 + 2 * b)[:, P * t:P * (t + 1)].rearrange("p (h c) -> p h c", h=H), ACT.Copy)
                    if t % 2 == 1:
                        cp.then_inc(v_copied, 1)
            act.wait_ge(v_mm, 3 * l + 3)
            for b in range(B):
                act.activation(vaugc[:, b, 0, :, 0:HD], bank(5)[:, 256 * b:256 * b + P].rearrange("p (h c) -> p h c", h=H),
                               ACT.Copy)
                act.activation(vaugc[0:CTX - P, b, 1, :, 0:HD],
                               bank(5)[0:CTX - P, 256 * b + P:256 * b + 2 * P].rearrange("p (h c) -> p h c", h=H),
                               ACT.Copy).then_inc(v_copied, 1)
            act_unit(act, l, 4, 0)
            act_unit(act, l, 4, 1)
            act_attention(act, l, 0)
            ln_act(act, c["ln"] + 3 * l + 1)
            act_unit(act, l, 5, 0)
            act_unit(act, l, 6, 0)
            act_unit(act, l, 5, 1)
            act_unit(act, l, 6, 1)
            act_attention(act, l, 1)
            ln_act(act, c["ln"] + 3 * l + 2)
            for f in range(B * FT):
                b, t = f // FT, f % FT
                act.wait_ge(hid_mm, B * FT * l + f + 1)
                act.activation(hid[:, t, b * S:(b + 1) * S], bank(4 + f % 4), ACT.Gelu, bias=bias[:, 6 + t:7 + t])\
                   .then_inc(hid_ready, 1)

        def dve_layer(ve, l, c):
            h_is(l, 0, c)(ve, 1)
            ve.tensor_copy(bias[:, 0:NBIAS], bias_all[:, bass.ds(l * NBIAS, NBIAS)]).then_inc(bias_copied, 1)
            ve.wait_ge(bias_copied, l + 1)
            ve.wait_ge(gain_mm, l + 1)
            raw = bank(4)[:, 0:12].rearrange("p (k w b) -> p k w b", k=3, w=2)
            bb = bias[:, 0:6].rearrange("p (k w) -> p k w", k=3)
            for b in range(B):
                ve.scalar_tensor_tensor(gains[:, :, 0, b], raw[:, :, 0, b], 1.0, bb[:, :, 0], ALU.add, ALU.add)\
                  .then_inc(gains_ready, 1)
                ve.tensor_tensor(gains[:, :, 1, b], raw[:, :, 1, b], bb[:, :, 1], ALU.add).then_inc(gains_ready, 1)
            ve.wait_ge(gains_ready, 4 * (l + 1))

            def norm(k):
                ln_dve(ve, c["ln"] + 3 * l + k, xn, gain=lambda b: gains[:, k, 0, b:b + 1],
                       shift=lambda b: gains[:, k, 1, b:b + 1], scaled=c["scaled"] + 3 * l + k)

            norm(0)
            for u in range(5):
                dve_unit(ve, l, u)
            dve_attention(ve, l, 0, c)
            norm(1)
            for u in (5, 6):
                dve_unit(ve, l, u)
            dve_attention(ve, l, 1, c)
            norm(2)
            for b in range(B):
                ve.wait_ge(out_mm, 6 * l + 4 + b + 1)
                ve.scalar_tensor_tensor(cols(h, b), bank(b), bias[:, 10:11], cols(h, b), ALU.add, ALU.add)\
                  .then_inc(h_ready, 1)

        def pool_layer(gp, l, c):
            for u in range(5):
                pool_unit(gp, l, u)
            pool_attention(gp, l, 0)
            for u in (5, 6):
                pool_unit(gp, l, u)
            pool_attention(gp, l, 1)

        def load_section(sp, l, s):
            a, b = SECTIONS[s]
            sp.dma_start(w[:, a:b], dram["weights"][bass.ds(l * P, P), a:b]).then_inc(w_loaded[s], 16)

        def sp_layer(sp, l, c):
            for u in range(5):
                sp_unit(sp, l, u)
            sp.wait_ge(gain_mm, l + 1)
            load_section(sp, l + 1, SEC_NORM)
            sp.wait_ge(v_mm, 3 * l + 3)
            load_section(sp, l + 1, SEC_SELF)
            sp_attention(sp, l, 0)
            sp.wait_ge(out_mm, 6 * l + 2)
            load_section(sp, l + 1, SEC_SOUT)
            for u in (5, 6):
                sp_unit(sp, l, u)
            load_section(sp, l + 1, SEC_CROSS)
            sp_attention(sp, l, 1)
            sp.wait_ge(out_mm, 6 * l + 4)
            load_section(sp, l + 1, SEC_COUT)
            sp.wait_ge(out_mm, 6 * l + 6)
            load_section(sp, l + 1, SEC_FFN)

        v_zeroed, mask_made, setup_eps, ident_ready = sem("v_zeroed"), sem("mask_made"), sem("setup_eps"), sem("ident_ready")
        mask_row = sb("mask_row", [B, S + CP], BF16)
        mask_words = sb("mask_words", [B, MASK_BYTES // 4], mybir.dt.uint32)
        mask_u8 = mask_words[:, :].bitcast(U8)
        SMALL = [("consts", consts[:, :]), ("rope", rope[:, :, :]), ("ctx", ctxT[:, :]), ("cond", condT[:, :]),
                 ("masks", mask_words[:, :])]
        LOADED = 16 * len(SMALL)

        def x_is(v):
            def wait(eng, b):
                if v == 0:
                    eng.wait_ge(x_loaded, 16)
                else:
                    eng.wait_ge(x_ready, 2 * (v - 1) + b + 1)
            return wait

        used[0] = 0
        w0 = carve(6 * P).rearrange("p (k n) -> p k n", k=6)
        vec0 = carve(16)
        bv_rows = carve(P)
        ctxn = carve(B * CTX)
        key0 = carve(B * CTX)
        val0 = carve(4 * P).rearrange("p (b k n) -> p b k n", b=B, k=KC)
        attn0 = carve(4 * S).rearrange("p (k n) -> p k n", k=4)
        q0 = carve(T)
        upd0 = carve(T)
        hid0 = carve(T)
        mx0, smx0, sum0, inv0 = (carve(8) for _ in range(4))
        (V_MU, V_SIG, V_KG, V_KB, V_QG, V_QB, V_MG, V_MB, V_PG, V_PB, V_BK, V_BQ, V_BU, V_B1, V_B2) = range(15)
        WK, WV, WQ, WU, W1, W2 = range(6)
        sigma0 = carve(8)
        ITERS = 3
        s0 = {k: sem("slot_" + k) for k in
              ("loaded", "zeroed", "kv_mm", "kv_out", "sigma", "slots", "q_mm", "q_out", "logit_mm", "max", "max_scaled",
               "exp", "sum_inv", "attn", "upd_mm", "col_log", "col_inv", "upd_out", "lin_mm", "lin_out", "resid")}
        PER_ITER_RESID = 6

        def vec(i):
            return vec0[:, i:i + 1]

        def key_rows(k):
            return P if k % 2 == 0 else CTX - P

        def slots_are(n):
            return lambda eng, b: eng.wait_ge(s0["slots"], 2 * n + b + 1)

        def b0_pe(pe, c):
            ln_pe(pe, c["ln"], x, x_is(c["x"]))
            ln_pe(pe, c["ln"] + 1, ctxT[:, :], lambda eng, b: eng.wait_ge(ln_done, 2 * c["done"] + 2), width=CTX)
            pe.wait_ge(s0["loaded"], 48)
            pe.wait_ge(ln_done, 2 * c["done"] + 4)
            pe.matmul(bank(4)[:, 0:B * CTX], w0[:, WK], ctxn, start=True, stop=True).then_inc(s0["kv_mm"], 1)
            for b in range(B):
                for k in range(KC):
                    n = key_rows(k)
                    mm = pe.matmul(bank(5)[0:n, (2 * b + k) * P:(2 * b + k + 1) * P],
                                   ctxn[:, b * CTX + k * P:b * CTX + k * P + n], w0[:, WV], start=True, stop=True)
            mm.then_inc(s0["kv_mm"], 1)
            for t in range(ITERS):
                n = c["ln"] + 2 + 3 * t
                d = 2 * (c["done"] + 2 + 2 * t)
                ln_pe(pe, n, h, slots_are(t))
                pe.wait_ge(s0["kv_out"], 2)
                for b in range(B):
                    pe.wait_ge(ln_done, d + b + 1)
                    pe.matmul(bank(4 + b), w0[:, WQ], cols(xn, b), start=True, stop=True).then_inc(s0["q_mm"], 1)
                pe.wait_ge(s0["q_out"], 2 * t + 2)
                for k in range(4):
                    b, n_rows = k // 2, key_rows(k)
                    pe.matmul(bank(4 + k)[0:n_rows, :], key0[:, b * CTX + (k % 2) * P:b * CTX + (k % 2) * P + n_rows],
                              cols(q0, b), start=True, stop=True).then_inc(s0["logit_mm"], 1)
                pe.wait_ge(s0["zeroed"], 2)
                pe.wait_ge(s0["attn"], 4 * t + 4)
                for b in range(B):
                    for k in range(KC):
                        pe.matmul(bank(4 + b), val0[:, b, k], attn0[:, 2 * b + k], start=(k == 0), stop=(k == 1))
                    for k in range(KC):
                        mm = pe.matmul(bank(6 + b), mean_w, attn0[:, 2 * b + k], start=(k == 0), stop=(k == 1))
                    mm.then_inc(s0["upd_mm"], 1)
                for b in range(B):
                    pe.wait_ge(s0["upd_out"], 2 * t + b + 1)
                    pe.matmul(bank(4 + b), w0[:, WU], cols(upd0, b), start=True, stop=True).then_inc(s0["lin_mm"], 1)
                ln_pe(pe, n + 1, h, lambda eng, b: eng.wait_ge(s0["resid"], PER_ITER_RESID * t + b + 1))
                for b in range(B):
                    pe.wait_ge(ln_done, d + 2 + b + 1)
                    pe.matmul(bank(4 + b), w0[:, W1], cols(xn, b), start=True, stop=True).then_inc(s0["lin_mm"], 1)
                for b in range(B):
                    pe.wait_ge(s0["lin_out"], 2 * t + b + 1)
                    pe.matmul(bank(6 + b), w0[:, W2], cols(hid0, b), start=True, stop=True).then_inc(s0["lin_mm"], 1)
                ln_pe(pe, n + 2, h, lambda eng, b: eng.wait_ge(s0["resid"], PER_ITER_RESID * t + 4 + b + 1))

        def b0_act(act, c):
            ln_act(act, c["ln"])
            act.wait_ge(s0["loaded"], 48)
            act.activation(sigma0[:, 0:1], vec(V_SIG), ACT.Exp).then_inc(s0["sigma"], 1)
            ln_act(act, c["ln"] + 1, width=CTX)
            act.wait_ge(s0["kv_mm"], 1)
            act.activation(key0, bank(4)[:, 0:B * CTX], ACT.Identity, bias=vec(V_BK)).then_inc(s0["kv_out"], 1)
            for t in range(ITERS):
                n = c["ln"] + 2 + 3 * t
                ln_act(act, n)
                for b in range(B):
                    act.wait_ge(s0["q_mm"], 2 * t + b + 1)
                    act.activation(cols(q0, b), bank(4 + b), ACT.Identity, bias=vec(V_BQ)).then_inc(s0["q_out"], 1)
                for k in range(4):
                    r = key_rows(k)
                    act.wait_ge(s0["max_scaled"], 4 * t + k + 1)
                    act.wait_ge(s0["zeroed"], 2)
                    act.activation(attn0[0:r, k], bank(4 + k)[0:r, :], ACT.Exp, bias=smx0[0:r, k:k + 1],
                                   scale=float(D) ** 0.5, accum_out=sum0[0:r, k:k + 1]).then_inc(s0["exp"], 1)
                for b in range(B):
                    act.wait_ge(s0["upd_mm"], 2 * t + b + 1)
                    act.activation(cols(lg, b), bank(6 + b), ACT.Ln).then_inc(s0["col_log"], 1)
                    act.wait_ge(s0["col_log"], 2 * t + b + 1)
                    act.activation(cols(rstd, b), cols(lg, b), ACT.Exp, scale=-1.0).then_inc(s0["col_inv"], 1)
                ln_act(act, n + 1)
                for b in range(B):
                    act.wait_ge(s0["lin_mm"], 6 * t + 2 + b + 1)
                    act.activation(cols(hid0, b), bank(4 + b), ACT.Gelu, bias=vec(V_B1)).then_inc(s0["lin_out"], 1)
                both_log_and_exp(act)
                ln_act(act, n + 2)

        def b0_dve(ve, c):
            ve.memset(val0[:, :, :, :], 0.0).then_inc(s0["zeroed"], 1)
            ve.memset(attn0[:, :, :], 0.0).then_inc(s0["zeroed"], 1)
            ln_dve(ve, c["ln"], xn)
            ve.wait_ge(s0["loaded"], 48)
            ln_dve(ve, c["ln"] + 1, ctxn, gain=lambda b: vec(V_KG), shift=lambda b: vec(V_KB), width=CTX,
                   scaled=c["scaled"])
            ve.wait_ge(s0["sigma"], 1)
            for b in range(B):
                ve.wait_ge(ln_done, 2 * c["done"] + b + 1)
                ve.tensor_scalar(cols(h, b), cols(xn, b), sigma0[:, 0:1], vec(V_MU), ALU.mult, ALU.add)\
                  .then_inc(s0["slots"], 1)
            ve.wait_ge(s0["kv_mm"], 2)
            ve.wait_ge(s0["zeroed"], 2)
            for k in range(4):
                r = key_rows(k)
                op = ve.tensor_tensor(val0[0:r, k // 2, k % 2], bank(5)[0:r, k * P:(k + 1) * P], bv_rows[0:r, :], ALU.add)
            op.then_inc(s0["kv_out"], 1)
            for t in range(ITERS):
                n = c["ln"] + 2 + 3 * t
                sc = c["scaled"] + 1 + 3 * t
                ln_dve(ve, n, xn, gain=lambda b: vec(V_QG), shift=lambda b: vec(V_QB), scaled=sc)
                for k in range(4):
                    r = key_rows(k)
                    ve.wait_ge(s0["logit_mm"], 4 * t + k + 1)
                    ve.tensor_reduce(mx0[0:r, k:k + 1], bank(4 + k)[0:r, :], AX.X, ALU.max, negate=True)\
                      .then_inc(s0["max"], 1)
                    ve.wait_ge(s0["max"], 4 * t + k + 1)
                    ve.tensor_scalar(smx0[0:r, k:k + 1], mx0[0:r, k:k + 1], float(D) ** 0.5, None, ALU.mult)\
                      .then_inc(s0["max_scaled"], 1)
                for k in range(4):
                    r = key_rows(k)
                    ve.wait_ge(s0["exp"], 4 * t + k + 1)
                    ve.reciprocal(inv0[0:r, k:k + 1], sum0[0:r, k:k + 1]).then_inc(s0["sum_inv"], 1)
                    ve.wait_ge(s0["sum_inv"], 4 * t + k + 1)
                    ve.tensor_scalar(attn0[0:r, k], attn0[0:r, k], inv0[0:r, k:k + 1], 1e-8, ALU.mult, ALU.add)\
                      .then_inc(s0["attn"], 1)
                for b in range(B):
                    ve.wait_ge(s0["col_inv"], 2 * t + b + 1)
                    ve.scalar_tensor_tensor(cols(upd0, b), bank(4 + b), 1.0 / P, cols(rstd, b), ALU.mult, ALU.mult)\
                      .then_inc(s0["upd_out"], 1)
                for b in range(B):
                    ve.wait_ge(s0["lin_mm"], 6 * t + b + 1)
                    ve.scalar_tensor_tensor(cols(h, b), bank(4 + b), vec(V_BU), cols(h, b), ALU.add, ALU.add)\
                      .then_inc(s0["resid"], 1)
                ln_dve(ve, n + 1, xn, gain=lambda b: vec(V_MG), shift=lambda b: vec(V_MB), scaled=sc + 1)
                for b in range(B):
                    ve.wait_ge(s0["lin_mm"], 6 * t + 4 + b + 1)
                    ve.scalar_tensor_tensor(cols(h, b), bank(6 + b), vec(V_B2), cols(h, b), ALU.add, ALU.add)\
                      .then_inc(s0["resid"], 1)
                for b in range(B):
                    ve.wait_ge(s0["resid"], PER_ITER_RESID * t + 2 + b + 1)
                    ve.tensor_scalar(cols(h, b), cols(h, b), condT[:, b:b + 1], None, ALU.add).then_inc(s0["resid"], 1)
                ln_dve(ve, n + 2, h, gain=lambda b: vec(V_PG), shift=lambda b: vec(V_PB), scaled=sc + 2,
                       done=s0["slots"])
            for b in range(B):
                ve.wait_ge(s0["slots"], 2 * ITERS + b + 1)
                ve.tensor_tensor(cols(x, b), cols(x, b), cols(h, b), ALU.add).then_inc(x_ready, 1)

        def b0_sp(sp, c):
            sp.dma_start(w0, dram["w0"].rearrange("p (k n) -> p k n", k=6)).then_inc(s0["loaded"], 16)
            sp.dma_start(vec0[:, 0:15], dram["vec0"]).then_inc(s0["loaded"], 16)
            sp.dma_start(bv_rows, dram["bv_rows"]).then_inc(s0["loaded"], 16)

        def nothing(eng, c):
            pass

        MOE_COLS = 2 * DFF + P + FT + 1
        used[0] = 0
        wexp = carve(2 * MOE_COLS).rearrange("p (r n) -> p r n", r=2)
        hide = carve(FT * T).rearrange("p (t n) -> p t n", t=FT)
        gate_rows = carve(T)
        wgate = carve(T)
        part_out = carve(T)
        acc = carve(T)
        moe_end = used[0]
        m = {k: sem("moe_" + k) for k in
             ("gate_rows", "hid_mm", "hid", "gate_mm", "gate", "out_mm", "weighted", "added", "start")}
        expert_loaded = [sem(f"expert_loaded{i}") for i in range(2)]
        MIX = {1: (8, "we1", ACT.Gelu, False), 7: (16, "we3", ACT.Gelu_apprx_tanh, True)}

        def moe_pe(pe, c, k):
            n = MIX[k][0]
            pe.wait_ge(m["gate_rows"], 2 * (c["mixes"] + 1))
            with pe.Fori(c["experts"] // 2, (c["experts"] + n) // 2) as q:
                for i in range(2):
                    e, we = 2 * q + i, wexp[:, i]
                    pe.wait_ge(expert_loaded[i], 16 * (q + 1))
                    for b in range(B):
                        pe.matmul(bank(6 + b), we[0:n, 2 * DFF:2 * DFF + P], gate_rows[0:n, b * S:(b + 1) * S],
                                  start=True, stop=True).then_inc(m["gate_mm"], 1)
                    for f in range(B * FT):
                        b, t = f // FT, f % FT
                        if f >= 4:
                            pe.wait_ge(m["hid"], B * FT * e + f - 3)
                        pe.matmul(bank(f % 4), we[:, P * t:P * (t + 1)], cols(xn, b), start=True, stop=True)\
                          .then_inc(m["hid_mm"], 1)
                    for b in range(B):
                        pe.wait_ge(m["hid"], B * FT * e + FT * (b + 1))
                        for t in range(FT):
                            mm = pe.matmul(bank(4 + b), we[:, DFF + P * t:DFF + P * (t + 1)],
                                           hide[:, t, b * S:(b + 1) * S], start=(t == 0), stop=(t == FT - 1))
                        mm.then_inc(m["out_mm"], 1)

        def moe_act(act, c, k):
            n, _, func, biased = MIX[k]
            with act.Fori(c["experts"] // 2, (c["experts"] + n) // 2) as q:
                for i in range(2):
                    e = 2 * q + i
                    for b in range(B):
                        act.wait_ge(m["gate_mm"], 2 * e + b + 1)
                        act.wait_ge(m["weighted"], 2 * e + b + 1)
                        act.activation(cols(wgate, b), bank(6 + b), ACT.Copy).then_inc(m["gate"], 1)
                    for f in range(B * FT):
                        b, t = f // FT, f % FT
                        act.wait_ge(m["hid_mm"], B * FT * e + f + 1)
                        at = 2 * DFF + P + t
                        if biased:
                            act.activation(hide[:, t, b * S:(b + 1) * S], bank(f % 4), func,
                                           bias=wexp[:, i, at:at + 1]).then_inc(m["hid"], 1)
                        else:
                            act.activation(hide[:, t, b * S:(b + 1) * S], bank(f % 4), func).then_inc(m["hid"], 1)

        def moe_start(ve, c):
            if c["mixes"] == 0:
                for b in range(B):
                    ve.memset(cols(part_out, b), 0.0).then_inc(m["weighted"], 1)
            ve.memset(acc, 0.0).then_inc(m["start"], 1)
            ve.wait_ge(m["start"], c["mixes"] + 1)

        def moe_dve(ve, c, k):
            n, _, _, biased = MIX[k]
            with ve.Fori(c["experts"] // 2, (c["experts"] + n) // 2) as q:
                for i in range(2):
                    e = 2 * q + i
                    for b in range(B):
                        ve.wait_ge(m["gate"], 2 * e + b + 1)
                        ve.wait_ge(m["out_mm"], 2 * e + b + 1)
                        if biased:
                            op = ve.scalar_tensor_tensor(cols(part_out, b), bank(4 + b), wexp[:, i, MOE_COLS - 1:MOE_COLS],
                                                         cols(wgate, b), ALU.add, ALU.mult)
                        else:
                            op = ve.tensor_tensor(cols(part_out, b), bank(4 + b), cols(wgate, b), ALU.mult)
                        op.then_inc(m["weighted"], 1)
                        ve.wait_ge(m["weighted"], 2 * e + 2 + b + 1)
                        ve.tensor_tensor(cols(acc, b), cols(acc, b), cols(part_out, b), ALU.add).then_inc(m["added"], 1)
            for b in range(B):
                ve.wait_ge(m["added"], 2 * (c["experts"] + n) - 1 + b)
                ve.tensor_tensor(cols(x, b), cols(x, b), cols(acc, b), ALU.add).then_inc(x_ready, 1)

        def moe_sp(sp, c, k):
            n, name = MIX[k][:2]
            x_is(c["x"])(sp, 1)
            for i in range(2):
                sp.dma_start(wexp[:, i], dram[name][P * i:P * (i + 1), :]).then_inc(expert_loaded[i], 16)
            with sp.Fori(0, n // 2 - 1) as q:
                for i in range(2):
                    sp.wait_ge(m["added"], 4 * q + 2 * (c["experts"] + i + 1))
                    sp.dma_start(wexp[:, i], dram[name][bass.ds(q * (2 * P) + (2 + i) * P, P), :])\
                      .then_inc(expert_loaded[i], 16)

        used[0] = moe_end
        rw1 = carve(8)
        iota8 = carve(8)
        route = carve(64).rearrange("p (t e) -> p t e", t=8)
        best = carve(64).rearrange("p (t e) -> p t e", t=8)
        which = carve(64, mybir.dt.uint32).rearrange("p (t e) -> p t e", t=8)
        whichf = carve(16).rearrange("p (t e) -> p t e", t=8)
        ratio = carve(8)
        ratio_e = carve(8)
        denom = carve(8)
        gate1 = carve(8)
        gate2 = carve(8)
        hot1, hot2, wsum = (carve(64).rearrange("p (t e) -> p t e", t=8) for _ in range(3))
        TT = T // P
        r1 = {k: sem("route_" + k) for k in ("loaded", "mm", "scores", "best", "which", "dve", "exp", "turned")}

        def over_experts(a):
            return a.unsqueeze(2).broadcast_to([P, TT, 8])

        def route_scores_pe(pe, uses):
            for t in range(TT):
                mm = pe.matmul(bank(0)[:, 8 * t:8 * t + 8], xn[:, P * t:P * (t + 1)], rw1, start=True, stop=True)
            mm.then_inc(r1["mm"], 1)

        def turn_gates_pe(pe, src):
            for t in range(TT):
                tr = pe.transpose(bank(2 + t // 4)[0:8, P * (t % 4):P * (t % 4 + 1)], src[:, t, :], ident)
            tr.then_inc(r1["turned"], 1)

        def b1_pe(pe, c):
            ln_pe(pe, c["ln"], x, x_is(c["x"]))
            pe.wait_ge(r1["loaded"], 32)
            pe.wait_ge(ln_done, 2 * c["done"] + 2)
            route_scores_pe(pe, 0)
            pe.wait_ge(r1["dve"], 9)
            turn_gates_pe(pe, wsum)
            moe_pe(pe, c, 1)

        def b1_act(act, c):
            ln_act(act, c["ln"])
            act.wait_ge(r1["dve"], 1)
            act.activation(ratio_e, ratio, ACT.Exp).then_inc(r1["exp"], 1)
            act.wait_ge(r1["turned"], 1)
            for b in range(B):
                act.activation(gate_rows[0:8, b * S:(b + 1) * S], bank(2 + b)[0:8, :], ACT.Copy)\
                   .then_inc(m["gate_rows"], 1)
            moe_act(act, c, 1)

        def b1_dve(ve, c):
            ln_dve(ve, c["ln"], xn)
            moe_start(ve, c)
            ve.wait_ge(r1["mm"], 1)
            ve.tensor_copy(route[:, :, :], bank(0)[:, 0:64].rearrange("p (t e) -> p t e", t=TT)).then_inc(r1["scores"], 1)
            ve.wait_ge(r1["scores"], 1)
            for t in range(TT):
                ve.max(best[:, t, :], route[:, t, :]).then_inc(r1["best"], 1)
            ve.wait_ge(r1["best"], TT)
            for t in range(TT):
                ve.max_index(which[:, t, :], best[:, t, :], route[:, t, :]).then_inc(r1["which"], 1)
            step = [0]

            def then(op):
                step[0] += 1
                op.then_inc(r1["dve"], 1)
                ve.wait_ge(r1["dve"], step[0])

            then(ve.tensor_tensor(ratio, best[:, :, 1], best[:, :, 0], ALU.subtract))
            ve.wait_ge(r1["exp"], 1)
            then(ve.tensor_scalar(denom, ratio_e, 1.0, None, ALU.add))
            then(ve.reciprocal(gate1, denom))
            then(ve.tensor_tensor(gate2, ratio_e, gate1, ALU.mult))
            ve.wait_ge(r1["which"], TT)
            then(ve.tensor_copy(whichf[:, :, :], which[:, :, 0:2]))
            iota = iota8.unsqueeze(1).broadcast_to([P, TT, 8])
            ve.wait_ge(r1["loaded"], 32)
            ve.tensor_tensor(hot1[:, :, :], iota, over_experts(whichf[:, :, 0]), ALU.is_equal)
            then(ve.tensor_tensor(hot2[:, :, :], iota, over_experts(whichf[:, :, 1]), ALU.is_equal))
            ve.tensor_tensor(hot1[:, :, :], hot1[:, :, :], over_experts(gate1), ALU.mult)
            then(ve.tensor_tensor(hot2[:, :, :], hot2[:, :, :], over_experts(gate2), ALU.mult))
            then(ve.tensor_tensor(wsum[:, :, :], hot1[:, :, :], hot2[:, :, :], ALU.add))
            then(ve.tensor_copy(whichf[:, :, 0], whichf[:, :, 1]))
            moe_dve(ve, c, 1)

        def b1_sp(sp, c):
            x_is(c["x"])(sp, 1)
            sp.dma_start(rw1, dram["rw1"]).then_inc(r1["loaded"], 16)
            sp.dma_start(iota8, dram["iota8"]).then_inc(r1["loaded"], 16)
            moe_sp(sp, c, 1)

        used[0] = 0
        HEADS2, DH2 = 16, 64
        KEYS2 = CTX + S
        KT2 = -(-KEYS2 // P)
        TAIL2 = KEYS2 - (KT2 - 1) * P
        kv2 = carve(B * KEYS2).rearrange("p (b n) -> p b n", b=B)
        wh2 = carve(2 * 320).rearrange("p (r n) -> p r n", r=2)
        vec2 = carve(8)
        cond1 = carve(8)
        gain2 = carve(8)
        shift2 = carve(8)
        qa2 = carve(B * S).rearrange("p (b n) -> p b n", b=B)
        ka2 = carve(B * KEYS2).rearrange("p (b n) -> p b n", b=B)
        va2 = carve(B * KT2 * 65).rearrange("p (b k c) -> p b k c", b=B, k=KT2)
        prob2 = carve(B * KT2 * S).rearrange("p (b k n) -> p b k n", b=B, k=KT2)
        nm2 = carve(8)
        osb2 = carve(B * S).rearrange("p (b n) -> p b n", b=B)
        dlog2 = carve(B * S).rearrange("p (b n) -> p b n", b=B)
        dinv2 = carve(B * S).rearrange("p (b n) -> p b n", b=B)
        att2 = carve(B * S).rearrange("p (b n) -> p b n", b=B)
        ones2 = carve(DH2)
        acc2 = carve(T)
        s2 = {k: sem("ctx_" + k) for k in
              ("loaded", "ready", "gain", "context", "qkv_mm", "q", "k", "v", "score_mm", "max", "row_mm", "row", "exp_mm",
               "exp", "pv_mm", "o", "den_mm", "den_log", "den_inv", "att", "out_mm", "acc")}
        w_head2 = [sem(f"w_head{i}") for i in range(2)]

        def tile_keys(j):
            return P if j < KT2 - 1 else TAIL2

        def b2_pe(pe, c):
            ln_pe(pe, c["ln"], x, x_is(c["x"]))
            ln_pe(pe, c["ln"] + 1, ctxT[:, :], lambda eng, b: eng.wait_ge(ln_done, 2 * c["done"] + 2), width=CTX)
            ln_pe(pe, c["ln"] + 2, h, lambda eng, b: eng.wait_ge(s2["context"], 2))
            pe.wait_ge(ln_done, 2 * c["done"] + 4)
            pe.wait_ge(s2["ready"], 5)
            with pe.Fori(0, HEADS2 // 2) as q:
                for i in range(2):
                    hh, wt = 2 * q + i, wh2[:, i]

                    def project(b):
                        o = 4 * b
                        pe.matmul(bank(o)[0:DH2, :], wt[:, 0:64], kv2[:, b, CTX:KEYS2], start=True, stop=True)
                        pe.matmul(bank(o + 1)[0:DH2, :], wt[:, 64:128], kv2[:, b, 0:S], start=True, stop=True)
                        pe.matmul(bank(o + 2)[0:DH2, 0:CTX], wt[:, 64:128], kv2[:, b, S:KEYS2], start=True, stop=True)
                        for j in range(KT2):
                            mm = pe.matmul(bank(o + 3)[0:tile_keys(j), 64 * j:64 * (j + 1)],
                                           kv2[:, b, P * j:P * j + tile_keys(j)], wt[:, 128:192], start=True, stop=True)
                        mm.then_inc(s2["qkv_mm"], 1)

                    def scores(b):
                        for name in ("q", "k", "v"):
                            pe.wait_ge(s2[name], 2 * hh + b + 1)
                        for t in range(4):
                            n = 4 * b + t
                            if n >= 2:
                                pe.wait_ge(s2["max"], 8 * hh + n - 1)
                            o = 2 * (n % 2)
                            lhs = qa2[0:DH2, b, P * t:P * (t + 1)]
                            pe.matmul(bank(o), lhs, ka2[0:DH2, b, 0:S], start=True, stop=True)
                            pe.matmul(bank(o + 1)[:, 0:CTX], lhs, ka2[0:DH2, b, S:KEYS2], start=True, stop=True)\
                              .then_inc(s2["score_mm"], 1)

                    def max_row2(b):
                        pe.wait_ge(s2["max"], 8 * hh + 4 * b + 4)
                        for t in range(4):
                            mm = pe.matmul(bank(4)[64:65, P * t:P * (t + 1)], nm2[:, 4 * b + t:4 * b + t + 1], ident,
                                           start=True, stop=True)
                        mm.then_inc(s2["row_mm"], 1)

                    def exp_tile(b, j):
                        k = 6 * b + j
                        if j == 0:
                            pe.wait_ge(s2["row"], 2 * hh + b + 1)
                        if k >= 2:
                            pe.wait_ge(s2["exp"], 12 * hh + k - 1)
                        n = tile_keys(j)
                        pe.matmul(bank(5 + k % 2)[0:n, :], ka2[0:65, b, P * j:P * j + n], qa2[0:65, b, :],
                                  start=True, stop=True).then_inc(s2["exp_mm"], 1)

                    def values(b, j):
                        pe.wait_ge(s2["exp"], 12 * hh + 6 * b + j + 1)
                        if j == 0 and b == 1:
                            pe.wait_ge(s2["o"], 2 * hh + 1)
                        mm = pe.matmul(bank(7)[0:65, :], va2[:, b, j], prob2[:, b, j], start=(j == 0), stop=(j == KT2 - 1))
                        if j == KT2 - 1:
                            mm.then_inc(s2["pv_mm"], 1)

                    def den2(b):
                        pe.wait_ge(s2["o"], 2 * hh + b + 1)
                        if b == 1:
                            pe.wait_ge(s2["acc"], 2 * hh + 3)
                        pe.matmul(bank(4)[0:DH2, :], ones2[64:65, 0:DH2], osb2[64:65, b, :], start=True, stop=True)\
                          .then_inc(s2["den_mm"], 1)

                    def out2(b):
                        pe.wait_ge(s2["att"], 2 * hh + b + 1)
                        pe.matmul(bank(4), wt[0:DH2, 192:320], att2[0:DH2, b, :], start=True, stop=True)\
                          .then_inc(s2["out_mm"], 1)

                    pe.wait_ge(w_head2[i], 16 * (q + 1))
                    project(0)
                    pe.wait_ge(s2["acc"], 2 * hh + 2)
                    project(1)
                    scores(0)
                    scores(1)
                    max_row2(0)
                    for j in range(KT2):
                        exp_tile(0, j)
                        if j >= 2:
                            values(0, j - 2)
                    pe.wait_ge(s2["row"], 2 * hh + 1)
                    max_row2(1)
                    values(0, 4)
                    values(0, 5)
                    for j in range(KT2):
                        exp_tile(1, j)
                        if j == 1:
                            den2(0)
                        if j >= 2:
                            values(1, j - 2)
                    out2(0)
                    values(1, 4)
                    values(1, 5)
                    den2(1)
                    out2(1)

        def b2_act(act, c):
            ln_act(act, c["ln"])
            ln_act(act, c["ln"] + 1, width=CTX)
            ln_act(act, c["ln"] + 2)
            with act.Fori(0, HEADS2 // 2) as q:
                for i in range(2):
                    hh = 2 * q + i

                    def row(b):
                        act.wait_ge(s2["row_mm"], 2 * hh + b + 1)
                        act.activation(qa2[64:65, b, :], bank(4)[64:65, :], ACT.Copy).then_inc(s2["row"], 1)

                    def exp(b, j):
                        k, n = 6 * b + j, tile_keys(j)
                        act.wait_ge(s2["exp_mm"], 12 * hh + k + 1)
                        act.activation(prob2[0:n, b, j], bank(5 + k % 2)[0:n, :], ACT.Exp, scale=DH2 ** -0.5)\
                           .then_inc(s2["exp"], 1)

                    def copy_o(b):
                        act.wait_ge(s2["pv_mm"], 2 * hh + b + 1)
                        act.activation(osb2[0:65, b, :], bank(7)[0:65, :], ACT.Copy).then_inc(s2["o"], 1)

                    def invert2(b):
                        act.wait_ge(s2["den_mm"], 2 * hh + b + 1)
                        act.activation(dlog2[0:DH2, b, :], bank(4)[0:DH2, :], ACT.Ln).then_inc(s2["den_log"], 1)
                        act.wait_ge(s2["den_log"], 2 * hh + b + 1)
                        act.activation(dinv2[0:DH2, b, :], dlog2[0:DH2, b, :], ACT.Exp, scale=-1.0)\
                           .then_inc(s2["den_inv"], 1)

                    for b in range(B):
                        act.wait_ge(s2["qkv_mm"], 2 * hh + b + 1)
                        act.activation(qa2[0:DH2, b, :], bank(4 * b)[0:DH2, :], ACT.Copy).then_inc(s2["q"], 1)
                        act.activation(ka2[0:DH2, b, :], bank(4 * b + 1, 2)[0:DH2, 0:KEYS2], ACT.Copy).then_inc(s2["k"], 1)
                    row(0)
                    for j in range(KT2):
                        exp(0, j)
                    row(1)
                    for j in range(KT2):
                        exp(1, j)
                        if j == 0:
                            copy_o(0)
                        if j == 3:
                            invert2(0)
                    copy_o(1)
                    invert2(1)

        def b2_dve(ve, c):
            x_is(c["x"])(ve, 1)
            ve.memset(va2[:, :, :, :], 0.0).then_inc(s2["ready"], 1)
            ve.memset(prob2[:, :, KT2 - 1, :], 0.0).then_inc(s2["ready"], 1)
            ve.wait_ge(s2["ready"], 2)
            ve.memset(va2[:, :, :, 64:65], 1.0).then_inc(s2["ready"], 1)
            ve.memset(ka2[64:65, :, :], 1.0).then_inc(s2["ready"], 1)
            ve.memset(ones2[64:65, :], 1.0).then_inc(s2["ready"], 1)
            ve.memset(cols(acc2, 0), 0.0).then_inc(s2["acc"], 1)
            ve.memset(cols(acc2, 1), 0.0).then_inc(s2["acc"], 1)
            ve.wait_ge(s2["loaded"], 16)
            ve.tensor_scalar(cond1[:, 0:B], condT[:, :], 1.0, None, ALU.add).then_inc(s2["gain"], 1)
            ve.wait_ge(s2["gain"], 1)
            ve.tensor_scalar(gain2[:, 0:B], cond1[:, 0:B], vec2[:, 2:3], None, ALU.mult).then_inc(s2["gain"], 1)
            ve.tensor_scalar(shift2[:, 2:2 + B], cond1[:, 0:B], vec2[:, 3:4], None, ALU.mult).then_inc(s2["gain"], 1)
            ve.wait_ge(s2["gain"], 3)
            ve.tensor_tensor(shift2[:, 0:B], shift2[:, 2:2 + B], condT[:, :], ALU.add).then_inc(s2["gain"], 1)
            ve.wait_ge(s2["gain"], 4)
            ln_dve(ve, c["ln"], h)
            ln_dve(ve, c["ln"] + 1, lambda b: kv2[:, b, 0:CTX], gain=lambda b: vec2[:, 0:1], shift=lambda b: vec2[:, 1:2],
                   width=CTX, scaled=c["scaled"], done=s2["context"])
            ln_dve(ve, c["ln"] + 2, lambda b: kv2[:, b, CTX:KEYS2], gain=lambda b: gain2[:, b:b + 1],
                   shift=lambda b: shift2[:, b:b + 1], scaled=c["scaled"] + 1)
            with ve.Fori(0, HEADS2 // 2) as q:
                for i in range(2):
                    hh = 2 * q + i
                    for b in range(B):
                        ve.wait_ge(s2["qkv_mm"], 2 * hh + b + 1)
                        v = bank(4 * b + 3)[:, 0:KT2 * 64].rearrange("p (k c) -> p k c", k=KT2)
                        ve.tensor_copy(va2[:, b, 0:KT2 - 1, 0:64], v[:, 0:KT2 - 1, :])
                        ve.tensor_copy(va2[0:TAIL2, b, KT2 - 1, 0:64], v[0:TAIL2, KT2 - 1, :]).then_inc(s2["v"], 1)
                    for n in range(8):
                        ve.wait_ge(s2["score_mm"], 8 * hh + n + 1)
                        ve.tensor_reduce(nm2[:, n:n + 1], bank(2 * (n % 2), 2)[:, 0:KEYS2], AX.X, ALU.max, negate=True)\
                          .then_inc(s2["max"], 1)
                    for b in range(B):
                        ve.wait_ge(s2["den_inv"], 2 * hh + b + 1)
                        ve.tensor_tensor(att2[0:DH2, b, :], osb2[0:DH2, b, :], dinv2[0:DH2, b, :], ALU.mult)\
                          .then_inc(s2["att"], 1)
                        ve.wait_ge(s2["out_mm"], 2 * hh + b + 1)
                        ve.wait_ge(s2["acc"], 2 * hh + b + 1)
                        ve.tensor_tensor(cols(acc2, b), bank(4), cols(acc2, b), ALU.add).then_inc(s2["acc"], 1)
            for b in range(B):
                ve.wait_ge(s2["acc"], 2 * HEADS2 + b + 1)
                ve.tensor_tensor(cols(x, b), cols(x, b), cols(acc2, b), ALU.add).then_inc(x_ready, 1)

        def b2_sp(sp, c):
            x_is(c["x"])(sp, 1)
            sp.dma_start(vec2[:, 0:4], dram["vec2"]).then_inc(s2["loaded"], 16)
            for i in range(2):
                sp.dma_start(wh2[:, i], dram["heads2"][P * i:P * (i + 1), :]).then_inc(w_head2[i], 16)
            with sp.Fori(0, HEADS2 // 2 - 1) as q:
                for i in range(2):
                    sp.wait_ge(s2["out_mm"], 4 * q + 2 * (i + 1))
                    sp.dma_start(wh2[:, i], dram["heads2"][bass.ds(q * (2 * P) + (2 + i) * P, P), :])\
                      .then_inc(w_head2[i], 16)

        used[0] = 0
        rw3 = carve(8)
        rb3 = carve(8)
        iota3 = carve(8)
        wa3 = carve(P)
        wb3 = carve(DFF)
        wi3 = carve(DFF)
        wo3 = carve(DFF).rearrange("p (t n) -> p t n", t=FT)
        spread3 = carve(P)
        vec3 = carve(8)
        route3, best3, hot3 = (carve(64).rearrange("p (t e) -> p t e", t=8) for _ in range(3))
        which3 = carve(64, mybir.dt.uint32).rearrange("p (t e) -> p t e", t=8)
        whichf3 = carve(8)
        mask3 = carve(T)
        low3 = carve(T)
        masked3 = carve(T)
        hid3 = carve(FT * T).rearrange("p (t n) -> p t n", t=FT)
        LOADS3 = 9
        TIMES3 = {"loaded": 16 * LOADS3, "route_mm": 1, "route": 1, "best": TT, "which": TT, "whichf": 1, "hot": 1,
                  "turned": 1, "mask": B, "spread_mm": B, "low_mm": B, "low": B, "masked": B, "hid_mm": B * FT,
                  "hid": B * FT, "out_mm": B}
        events = [sem("low_" + k) for k in TIMES3]
        s3 = dict(zip(TIMES3, events))
        spent3 = [n if FIRST <= 3 <= LAST else 0 for n in TIMES3.values()]

        def b3_pe(pe, c):
            ln_pe(pe, c["ln"], x, x_is(c["x"]))
            pe.wait_ge(s3["loaded"], 16 * LOADS3)
            pe.wait_ge(ln_done, 2 * c["done"] + 2)
            for t in range(TT):
                mm = pe.matmul(bank(0)[:, 8 * t:8 * t + 8], xn[:, P * t:P * (t + 1)], rw3, start=True, stop=True)
            mm.then_inc(s3["route_mm"], 1)
            for b in range(B):
                pe.matmul(bank(4 + b), wa3, cols(xn, b), start=True, stop=True).then_inc(s3["low_mm"], 1)
            pe.wait_ge(s3["hot"], 1)
            for t in range(TT):
                tr = pe.transpose(bank(2 + t // 4)[0:8, P * (t % 4):P * (t % 4 + 1)], hot3[:, t, :], ident)
            tr.then_inc(s3["turned"], 1)
            for b in range(B):
                pe.wait_ge(s3["mask"], b + 1)
                pe.matmul(bank(6 + b), spread3[0:8, :], mask3[0:8, b * S:(b + 1) * S], start=True, stop=True)\
                  .then_inc(s3["spread_mm"], 1)
            for f in range(B * FT):
                b, t = f // FT, f % FT
                pe.wait_ge(s3["masked"], b + 1)
                if f >= 4:
                    pe.wait_ge(s3["hid"], f - 3)
                elif f >= 2:
                    pe.wait_ge(s3["mask"], 2)
                pe.matmul(bank(f % 4), wi3[:, P * t:P * (t + 1)], cols(xn, b), start=True, stop=False)
                pe.matmul(bank(f % 4), wb3[:, P * t:P * (t + 1)], cols(masked3, b), start=False, stop=True)\
                  .then_inc(s3["hid_mm"], 1)
            for b in range(B):
                pe.wait_ge(s3["hid"], FT * (b + 1))
                for t in range(FT):
                    mm = pe.matmul(bank(4 + b), wo3[:, t], hid3[:, t, b * S:(b + 1) * S], start=(t == 0),
                                   stop=(t == FT - 1))
                mm.then_inc(s3["out_mm"], 1)

        def b3_act(act, c):
            ln_act(act, c["ln"])
            for b in range(B):
                act.wait_ge(s3["low_mm"], b + 1)
                act.activation(cols(low3, b), bank(4 + b), ACT.Copy).then_inc(s3["low"], 1)
            for b in range(B):
                act.wait_ge(s3["turned"], 1)
                act.activation(mask3[0:8, b * S:(b + 1) * S], bank(2 + b)[0:8, :], ACT.Copy).then_inc(s3["mask"], 1)
            act.wait_ge(s3["loaded"], 16 * LOADS3)
            for f in range(B * FT):
                b, t = f // FT, f % FT
                act.wait_ge(s3["hid_mm"], f + 1)
                act.activation(hid3[:, t, b * S:(b + 1) * S], bank(f % 4), ACT.Relu, bias=vec3[:, t:t + 1])\
                   .then_inc(s3["hid"], 1)

        def b3_dve(ve, c):
            ln_dve(ve, c["ln"], xn)
            ve.wait_ge(s3["loaded"], 16 * LOADS3)
            ve.wait_ge(s3["route_mm"], 1)
            ve.tensor_tensor(route3[:, :, :], bank(0)[:, 0:64].rearrange("p (t e) -> p t e", t=TT),
                             rb3.unsqueeze(1).broadcast_to([P, TT, 8]), ALU.add).then_inc(s3["route"], 1)
            ve.wait_ge(s3["route"], 1)
            for t in range(TT):
                ve.max(best3[:, t, :], route3[:, t, :]).then_inc(s3["best"], 1)
            ve.wait_ge(s3["best"], TT)
            for t in range(TT):
                ve.max_index(which3[:, t, :], best3[:, t, :], route3[:, t, :]).then_inc(s3["which"], 1)
            ve.wait_ge(s3["which"], TT)
            ve.tensor_copy(whichf3, which3[:, :, 0]).then_inc(s3["whichf"], 1)
            ve.wait_ge(s3["whichf"], 1)
            ve.tensor_tensor(hot3[:, :, :], iota3.unsqueeze(1).broadcast_to([P, TT, 8]), over_experts(whichf3),
                             ALU.is_equal).then_inc(s3["hot"], 1)
            for b in range(B):
                ve.wait_ge(s3["low"], b + 1)
                ve.wait_ge(s3["spread_mm"], b + 1)
                ve.tensor_tensor(cols(masked3, b), bank(6 + b), cols(low3, b), ALU.mult).then_inc(s3["masked"], 1)
            for b in range(B):
                ve.wait_ge(s3["out_mm"], b + 1)
                ve.scalar_tensor_tensor(cols(x, b), bank(4 + b), vec3[:, 4:5], cols(x, b), ALU.add, ALU.add)\
                  .then_inc(x_ready, 1)

        def b3_sp(sp, c):
            x_is(c["x"])(sp, 1)
            for name, dst in (("rw3", rw3), ("rb3", rb3), ("iota8", iota3), ("wa3", wa3), ("wb3", wb3), ("wi3", wi3),
                              ("wo3", wo3[:, :, :]), ("spread3", spread3), ("vec3", vec3[:, 0:5])):
                src = dram[name].rearrange("p (t n) -> p t n", t=FT) if name == "wo3" else dram[name]
                sp.dma_start(dst[0:8, :] if name == "spread3" else dst, src).then_inc(s3["loaded"], 16)

        used[0] = 0
        FI = 3
        WT5 = 2 * FI + FI
        NB5 = WT5 * P // 32
        wq5 = carve(WT5 * P)
        wr5 = carve(WT5 * P)
        wt5 = carve(WT5 * P).rearrange("p (t n) -> p t n", t=WT5)
        bmax5, bscale5, binv5 = (carve(NB5) for _ in range(3))
        xq5 = carve(T)
        up5, gate5, sig5 = (carve(FI * T) for _ in range(3))
        amax5 = carve(8)
        allmax5 = carve(8)
        scale5 = carve(8)
        inv5 = carve(8)
        MAGIC = 12582912.0
        STEPS5 = 3 + 3 + 3 + 3 + 1 + 3 + 1 + 3
        TIMES5 = {"loaded": 48, "w_dve": 7, "turned": 1, "w_ready": 3, "dve": STEPS5, "x_max": 15, "all_max": 5,
                  "up_mm": 2 * FI * B, "up": 2 * FI * B, "sigmoid": 1, "out_mm": B}
        s5 = dict(zip(TIMES5, events))
        at5 = dict(zip(TIMES5, spent3))
        spent5 = [a + (list(TIMES5.values())[i] if i < len(TIMES5) and FIRST <= 5 <= LAST else 0)
                  for i, a in enumerate(spent3)]

        def b5_pe(pe, c):
            pe.wait_ge(s5["w_dve"], at5["w_dve"] + 7)
            for t in range(WT5):
                tr = pe.transpose(bank(4 + t // 4)[:, P * (t % 4):P * (t % 4 + 1)], wq5[:, P * t:P * (t + 1)], ident)
            tr.then_inc(s5["turned"], 1)
            ln_pe(pe, c["ln"], x, x_is(c["x"]))
            pe.wait_ge(s5["w_ready"], at5["w_ready"] + 3)
            pe.wait_ge(s5["dve"], at5["dve"] + 3)
            for f in range(2 * FI * B):
                kind, t, b = f // (FI * B), f % (FI * B) // B, f % B
                if f >= 4:
                    pe.wait_ge(s5["up"], at5["up"] + f - 3)
                pe.matmul(bank(f % 4), wt5[:, (FI if kind == 0 else 0) + t], cols(xq5, b), start=True, stop=True)\
                  .then_inc(s5["up_mm"], 1)
            pe.wait_ge(s5["dve"], at5["dve"] + STEPS5)
            for b in range(B):
                for t in range(FI):
                    mm = pe.matmul(bank(4 + b), wt5[:, 2 * FI + t], up5[:, t * T + b * S:t * T + (b + 1) * S],
                                   start=(t == 0), stop=(t == FI - 1))
                mm.then_inc(s5["out_mm"], 1)

        def b5_act(act, c):
            act.wait_ge(s5["turned"], at5["turned"] + 1)
            for k in range(3):
                n = min(4, WT5 - 4 * k)
                act.activation(wt5[:, 4 * k:4 * k + n], bank(4 + k)[:, 0:n * P].rearrange("p (t n) -> p t n", n=P),
                               ACT.Copy).then_inc(s5["w_ready"], 1)
            ln_act(act, c["ln"])
            for f in range(2 * FI * B):
                kind, t, b = f // (FI * B), f % (FI * B) // B, f % B
                act.wait_ge(s5["up_mm"], at5["up_mm"] + f + 1)
                dst = (up5, gate5)[kind]
                act.activation(dst[:, t * T + b * S:t * T + (b + 1) * S], bank(f % 4), ACT.Copy).then_inc(s5["up"], 1)
            act.wait_ge(s5["dve"], at5["dve"] + 9)
            act.activation(sig5, gate5, ACT.Sigmoid).then_inc(s5["sigmoid"], 1)

        def b5_dve(ve, c):
            step = [0]

            def then(op):
                step[0] += 1
                op.then_inc(s5["dve"], 1)
                ve.wait_ge(s5["dve"], at5["dve"] + step[0])

            wstep = [0]

            def wthen(op):
                wstep[0] += 1
                op.then_inc(s5["w_dve"], 1)
                ve.wait_ge(s5["w_dve"], at5["w_dve"] + wstep[0])

            ve.wait_ge(s5["loaded"], at5["loaded"] + 48)
            blocks = lambda a: a.rearrange("p (k n) -> p k n", n=32)
            per_block = lambda a: a.unsqueeze(2).broadcast_to([P, NB5, 32])
            wthen(ve.tensor_reduce(bmax5, blocks(wq5), AX.X, ALU.max, apply_absolute_value=True))
            wthen(ve.tensor_scalar(bscale5, bmax5, float(np.float32(1 / 7)), 1e-12, ALU.mult, ALU.max))
            wthen(ve.reciprocal(binv5, bscale5))
            wthen(ve.tensor_tensor(blocks(wr5), blocks(wq5), per_block(binv5), ALU.mult))
            wthen(ve.tensor_scalar(wr5, wr5, MAGIC, MAGIC, ALU.add, ALU.subtract))
            wthen(ve.tensor_scalar(wr5, wr5, -8.0, 7.0, ALU.max, ALU.min))
            wthen(ve.tensor_tensor(blocks(wq5), blocks(wr5), per_block(bscale5), ALU.mult))
            ln_dve(ve, c["ln"], xq5)

            def quantise(k, a):
                ve.tensor_reduce(amax5[:, k:k + 1], a, AX.X, ALU.max, apply_absolute_value=True).then_inc(s5["x_max"], 1)
                ve.wait_ge(s5["all_max"], at5["all_max"] + k + 1)
                ve.tensor_scalar(scale5[:, k:k + 1], allmax5[:, k:k + 1], float(np.float32(1 / 32767)), 1e-12,
                                 ALU.mult, ALU.max).then_inc(s5["x_max"], 1)
                ve.wait_ge(s5["x_max"], at5["x_max"] + 3 * k + 2)
                ve.reciprocal(inv5[:, k:k + 1], scale5[:, k:k + 1]).then_inc(s5["x_max"], 1)
                ve.wait_ge(s5["x_max"], at5["x_max"] + 3 * k + 3)
                then(ve.tensor_scalar(a, a, inv5[:, k:k + 1], MAGIC, ALU.mult, ALU.add))
                then(ve.tensor_scalar(a, a, MAGIC, 32767.0, ALU.subtract, ALU.min))
                then(ve.tensor_scalar(a, a, -32768.0, scale5[:, k:k + 1], ALU.max, ALU.mult))

            ve.wait_ge(ln_done, 2 * c["done"] + 2)
            quantise(0, xq5)
            ve.wait_ge(s5["up"], at5["up"] + FI * B)
            quantise(1, up5)
            ve.wait_ge(s5["up"], at5["up"] + 2 * FI * B)
            quantise(2, gate5)
            ve.wait_ge(s5["sigmoid"], at5["sigmoid"] + 1)
            then(ve.tensor_scalar(sig5, sig5, 65536.0, MAGIC, ALU.mult, ALU.add))
            then(ve.tensor_scalar(sig5, sig5, MAGIC, 65535.0, ALU.subtract, ALU.min))
            then(ve.tensor_scalar(sig5, sig5, 0.0, 1.0 / 65536.0, ALU.max, ALU.mult))
            then(ve.tensor_tensor(gate5, gate5, sig5, ALU.mult))
            quantise(3, gate5)
            then(ve.tensor_tensor(up5, gate5, up5, ALU.mult))
            quantise(4, up5)
            for b in range(B):
                ve.wait_ge(s5["out_mm"], at5["out_mm"] + b + 1)
                ve.tensor_tensor(cols(x, b), bank(4 + b), cols(x, b), ALU.add).then_inc(x_ready, 1)

        def b5_pool(gp, c):
            for k in range(5):
                gp.wait_ge(s5["x_max"], at5["x_max"] + 3 * k + 1)
                gp.partition_all_reduce(allmax5[:, k:k + 1], amax5[:, k:k + 1], P, bass.bass_isa.ReduceOp.max)\
                  .then_inc(s5["all_max"], 1)

        def b5_sp(sp, c):
            x_is(c["x"])(sp, 1)
            sp.dma_start(wq5[:, 0:FI * P].rearrange("p (t n) -> p t n", t=FI),
                         dram["wg5"].rearrange("(t p) n -> p t n", p=P)).then_inc(s5["loaded"], 16)
            sp.dma_start(wq5[:, FI * P:2 * FI * P].rearrange("p (t n) -> p t n", t=FI),
                         dram["wu5"].rearrange("(t p) n -> p t n", p=P)).then_inc(s5["loaded"], 16)
            sp.dma_start(wq5[:, 2 * FI * P:], dram["wd5"]).then_inc(s5["loaded"], 16)

        used[0] = moe_end
        E7, ROUNDS, CAPACITY = 16, 6, 32
        gq7 = carve(E7)
        temp7 = carve(8)
        coef7 = carve(8)
        te = carve(T)
        pick7 = carve(T)
        junk7 = carve(T)
        tt7, et7 = (carve(TT * E7).rearrange("p (t e) -> p t e", t=TT) for _ in range(2))
        tmax7, tsum7, tlog7 = (carve(TT) for _ in range(3))
        emax7, esum7, elog7, ecor7 = (carve(8) for _ in range(4))
        top7 = carve(8)
        EVENTS7 = ("loaded", "coef", "logit_mm", "logits", "to_tokens", "t_dve", "t_exp", "t_log", "to_experts",
                   "e_max", "e_exp", "e_log", "e_dve", "affinity", "pick")
        s7 = dict(zip(EVENTS7, events))
        at7 = dict(zip(EVENTS7, spent5))

        def b7_pe(pe, c):
            ln_pe(pe, c["ln"], x, x_is(c["x"]))
            pe.wait_ge(s7["loaded"], at7["loaded"] + 32)
            for b in range(B):
                pe.wait_ge(ln_done, 2 * c["done"] + b + 1)
                pe.matmul(bank(4 + b)[0:E7, :], gq7, cols(xn, b), start=True, stop=True).then_inc(s7["logit_mm"], 1)
            for r in range(ROUNDS):
                if r == 0:
                    pe.wait_ge(s7["logits"], at7["logits"] + 2)
                else:
                    pe.wait_ge(s7["e_dve"], at7["e_dve"] + 4 * r)
                for t in range(TT):
                    tr = pe.transpose(bank(2)[:, E7 * t:E7 * (t + 1)], te[0:E7, P * t:P * (t + 1)], ident[0:E7, 0:E7])
                tr.then_inc(s7["to_tokens"], 1)
                pe.wait_ge(s7["t_dve"], at7["t_dve"] + 4 * r + 4)
                for t in range(TT):
                    tr = pe.transpose(bank(t // 4)[0:E7, P * (t % 4):P * (t % 4 + 1)], tt7[:, t, :], ident)
                tr.then_inc(s7["to_experts"], 1)
            moe_pe(pe, c, 7)

        def b7_act(act, c):
            act.wait_ge(s7["loaded"], at7["loaded"] + 32)
            act.activation(coef7[0:E7, 0:1], temp7[0:E7, 0:1], ACT.Exp, scale=-1.0).then_inc(s7["coef"], 1)
            ln_act(act, c["ln"])
            for r in range(ROUNDS):
                act.wait_ge(s7["t_dve"], at7["t_dve"] + 4 * r + 2)
                act.activation(et7[:, :, :], tt7[:, :, :], ACT.Exp).then_inc(s7["t_exp"], 1)
                act.wait_ge(s7["t_dve"], at7["t_dve"] + 4 * r + 3)
                act.activation(tlog7, tsum7, ACT.Ln).then_inc(s7["t_log"], 1)
                for b in range(B):
                    act.wait_ge(s7["e_max"], at7["e_max"] + 2 * r + b + 1)
                    act.activation(junk7[0:E7, b * S:(b + 1) * S], bank(b)[0:E7, :], ACT.Exp, bias=emax7[0:E7, b:b + 1],
                                   accum_out=esum7[0:E7, b:b + 1]).then_inc(s7["e_exp"], 1)
                act.wait_ge(s7["e_exp"], at7["e_exp"] + 2 * r + 2)
                act.activation(elog7[0:E7, 0:B], esum7[0:E7, 0:B], ACT.Ln).then_inc(s7["e_log"], 1)
            act.wait_ge(s7["e_dve"], at7["e_dve"] + 4 * ROUNDS)
            act.activation(pick7[0:E7, :], te[0:E7, :], ACT.Exp).then_inc(s7["affinity"], 1)
            act.wait_ge(s7["e_exp"], at7["e_exp"] + 2 * ROUNDS)
            act.activation(junk7[0:E7, :], te[0:E7, :], ACT.Exp).then_inc(s7["affinity"], 1)
            moe_act(act, c, 7)

        def b7_dve(ve, c):
            ln_dve(ve, c["ln"], xn)
            moe_start(ve, c)
            ve.wait_ge(s7["coef"], at7["coef"] + 1)
            for b in range(B):
                ve.wait_ge(s7["logit_mm"], at7["logit_mm"] + b + 1)
                ve.tensor_scalar(te[0:E7, b * S:(b + 1) * S], bank(4 + b)[0:E7, :], coef7[0:E7, 0:1], None, ALU.mult)\
                  .then_inc(s7["logits"], 1)
            for r in range(ROUNDS):
                ve.wait_ge(s7["to_tokens"], at7["to_tokens"] + r + 1)
                turned = bank(2)[:, 0:TT * E7].rearrange("p (t e) -> p t e", t=TT)
                wide = lambda a: a.unsqueeze(2).broadcast_to([P, TT, E7])
                ve.tensor_reduce(tmax7, turned, AX.X, ALU.max).then_inc(s7["t_dve"], 1)
                ve.wait_ge(s7["t_dve"], at7["t_dve"] + 4 * r + 1)
                ve.tensor_tensor(tt7[:, :, :], turned, wide(tmax7), ALU.subtract).then_inc(s7["t_dve"], 1)
                ve.wait_ge(s7["t_exp"], at7["t_exp"] + r + 1)
                ve.tensor_reduce(tsum7, et7[:, :, :], AX.X, ALU.add).then_inc(s7["t_dve"], 1)
                ve.wait_ge(s7["t_log"], at7["t_log"] + r + 1)
                ve.tensor_tensor(tt7[:, :, :], tt7[:, :, :], wide(tlog7), ALU.subtract).then_inc(s7["t_dve"], 1)
                ve.wait_ge(s7["to_experts"], at7["to_experts"] + r + 1)
                for b in range(B):
                    ve.tensor_reduce(emax7[0:E7, b:b + 1], bank(b)[0:E7, :], AX.X, ALU.max, negate=True)\
                      .then_inc(s7["e_max"], 1)
                ve.wait_ge(s7["e_log"], at7["e_log"] + r + 1)
                ve.wait_ge(s7["e_max"], at7["e_max"] + 2 * r + 2)
                ve.tensor_tensor(ecor7[0:E7, 0:B], emax7[0:E7, 0:B], elog7[0:E7, 0:B], ALU.subtract)\
                  .then_inc(s7["e_dve"], 1)
                ve.wait_ge(s7["e_dve"], at7["e_dve"] + 4 * r + 1)
                for b in range(B):
                    op = ve.tensor_scalar(te[0:E7, b * S:(b + 1) * S], bank(b)[0:E7, :], ecor7[0:E7, b:b + 1], None,
                                          ALU.add)
                    op.then_inc(s7["e_dve"], 1)
                ve.tensor_copy(elog7[0:E7, B:B + 1], elog7[0:E7, 0:1]).then_inc(s7["e_dve"], 1)
            ve.wait_ge(s7["affinity"], at7["affinity"] + 2)
            n = 0
            for b in range(B):
                part = pick7[0:E7, b * S:(b + 1) * S]
                for _ in range(CAPACITY // 8):
                    ve.max(top7[0:E7, :], part).then_inc(s7["pick"], 1)
                    n += 1
                    ve.wait_ge(s7["pick"], at7["pick"] + n)
                    ve.match_replace(part, top7[0:E7, :], part, -1.0).then_inc(s7["pick"], 1)
                    n += 1
                    ve.wait_ge(s7["pick"], at7["pick"] + n)
            for b in range(B):
                r = slice(b * S, (b + 1) * S)
                ve.scalar_tensor_tensor(gate_rows[0:E7, r], pick7[0:E7, r], 0.0, junk7[0:E7, r], ALU.is_lt, ALU.mult)\
                  .then_inc(m["gate_rows"], 1)
            moe_dve(ve, c, 7)

        def b7_sp(sp, c):
            x_is(c["x"])(sp, 1)
            sp.dma_start(gq7, dram["gq7"]).then_inc(s7["loaded"], 16)
            sp.dma_start(temp7[0:E7, 0:1], dram["temp7"]).then_inc(s7["loaded"], 16)
            moe_sp(sp, c, 7)

        def stack_pe(pe, c):
            ln_pe(pe, c["ln"] + 3 * c["layer"] - 1, x, x_is(c["x"]))
            pe.wait_ge(setup_done, c["setup"])
            pe.wait_ge(const_rows, 16 * 2 * B * c["stacks"])
            pe.wait_ge(loaded, LOADED)
            with pe.Fori(c["layer"], c["layer"] + NL) as l:
                pe_layer(pe, l, c)

        def stack_act(act, c):
            ln_act(act, c["ln"] + 3 * c["layer"] - 1)
            act.wait_ge(setup_done, c["setup"])
            with act.Fori(c["layer"], c["layer"] + NL) as l:
                act_layer(act, l, c)

        def stack_dve(ve, c):
            x_is(c["x"])(ve, 1)
            ve.memset(vaug[:, :, :, :, :], 0.0).then_inc(v_zeroed, 1)
            ve.memset(vaugc[:, :, :, :, :], 0.0).then_inc(v_zeroed, 1)
            ve.wait_ge(v_zeroed, 2 * c["stacks"])
            ve.memset(vaug[:, :, :, :, HD:HD + 1], 1.0).then_inc(setup_done, 1)
            ve.memset(vaugc[:, :, :, :, HD:HD + 1], 1.0).then_inc(setup_done, 1)
            ln_dve(ve, c["ln"] + 3 * c["layer"] - 1, h, done=h_ready)
            ve.wait_ge(bias_loaded, 16)
            with ve.Fori(c["layer"], c["layer"] + NL) as l:
                dve_layer(ve, l, c)
            for b in range(B):
                ve.wait_ge(h_ready, c["h"] + 6 * (c["layer"] + NL) - 2 + b + 1)
                ve.tensor_tensor(cols(x, b), cols(x, b), cols(h, b), ALU.add).then_inc(x_ready, 1)

        def stack_pool(gp, c):
            x_is(c["x"])(gp, 1)
            for a in (qst, kst, kstc):
                gp.memset(a[:, :, :], 1.0).then_inc(setup_done, 1)
            if c["stacks"] == 1:
                gp.wait_ge(loaded, LOADED)
                for dst, src in ((mask_row[:, 0:S], mask_u8[:, 0:S]), (mask_row[:, S:S + CTX], mask_u8[:, S:S + CTX])):
                    gp.tensor_scalar(dst, src, NEG, 10.0, ALU.mult, ALU.mult).then_inc(mask_made, 1)
                gp.memset(mask_row[:, S + CTX:S + CP], NEG).then_inc(mask_made, 1)
            with gp.Fori(c["layer"], c["layer"] + NL) as l:
                pool_layer(gp, l, c)

        def stack_sp(sp, c):
            sp.wait_ge(setup_done, c["setup"])
            sp.wait_ge(mask_made, 3)
            for b in range(B):
                sp.dma_start(kst[64 * b + ROW_MASK:64 * b + ROW_MASK + 1, :, :],
                             mask_row[b:b + 1, 0:S].unsqueeze(1).broadcast_to([1, H, S])).then_inc(const_rows, 16)
                sp.dma_start(kstc[64 * b + ROW_MASK:64 * b + ROW_MASK + 1, :, :],
                             mask_row[b:b + 1, S:S + CP].unsqueeze(1).broadcast_to([1, H, CP])).then_inc(const_rows, 16)
            with sp.Fori(c["layer"], c["layer"] + NL) as l:
                sp_layer(sp, l, c)

        RUN = {4: (stack_pe, stack_act, stack_dve, stack_pool, stack_sp),
               6: (stack_pe, stack_act, stack_dve, stack_pool, stack_sp),
               0: (b0_pe, b0_act, b0_dve, nothing, b0_sp), 1: (b1_pe, b1_act, b1_dve, nothing, b1_sp),
               2: (b2_pe, b2_act, b2_dve, nothing, b2_sp),
               3: (b3_pe, b3_act, b3_dve, nothing, b3_sp), 5: (b5_pe, b5_act, b5_dve, b5_pool, b5_sp),
               7: (b7_pe, b7_act, b7_dve, nothing, b7_sp)}
        USES = {0: {"ln": 11, "done": 2 + 2 * ITERS, "scaled": 1 + 3 * ITERS}, 1: {"ln": 1, "done": 1, "experts": 8, "mixes": 1},
                2: {"ln": 3, "done": 2, "scaled": 2}, 3: {"ln": 1, "done": 1}, 5: {"ln": 1, "done": 1}, 7: {"ln": 1, "done": 1, "experts": 16, "mixes": 1}}
        counts = {}
        c = {"ln": 0, "done": 0, "scaled": 0, "h": 0, "x": 0, "layer": 0, "stacks": 0, "setup": 0, "experts": 0, "mixes": 0}
        for k in range(FIRST, LAST + 1):
            if k in (4, 6):
                c["ln"] += 1
                c["h"] += 2
                c["stacks"] += 1
                c["setup"] += 5
                counts[k] = {**c, "ln": c["ln"] - 3 * c["layer"], "done": c["done"] - 3 * c["layer"],
                             "scaled": c["scaled"] - 3 * c["layer"]}
                c["ln"] += 3 * NL
                c["done"] += 3 * NL
                c["scaled"] += 3 * NL
                c["layer"] += NL
            else:
                counts[k] = dict(c)
                for name, n in USES[k].items():
                    c[name] += n
            c["x"] += 1

        block = ctx.enter_context(nc.Block())

        @block.tensor
        def _(pe):
            pe.wait_ge(loaded, LOADED)
            pe.wait_ge(ident_ready, 1)
            for k in counts:
                RUN[k][0](pe, counts[k])

        @block.scalar
        def _(act):
            act.wait_ge(loaded, LOADED)
            act.wait_ge(ident_ready, 1)
            for k in counts:
                both_log_and_exp(act)
                RUN[k][1](act, counts[k])

        @block.vector
        def _(ve):
            ve.memset(epst[:, :], EPS).then_inc(setup_eps, 1)
            ve.wait_ge(loaded, LOADED)
            ve.wait_ge(setup_eps, 2)
            ve.tensor_copy(identb[:, :], ident).then_inc(ident_ready, 1)
            for k in counts:
                RUN[k][2](ve, counts[k])

        @block.gpsimd
        def _(gp):
            gp.memset(zeros[:, :], 0.0).then_inc(setup_eps, 1)
            gp.wait_ge(setup_eps, 2)
            for k in counts:
                RUN[k][3](gp, counts[k])

        @block.sync
        def _(sp):
            sp.dma_start(x[:, :], dram["x"]).then_inc(x_loaded, 16)
            for name, dst in SMALL:
                sp.dma_start(dst, dram[name]).then_inc(loaded, 16)
            sp.dma_start(bias_all[:, :], dram["biases"]).then_inc(bias_loaded, 16)
            for s, (a, b) in enumerate(SECTIONS):
                sp.dma_start(w[:, a:b], dram["weights"][0:P, a:b]).then_inc(w_loaded[s], 16)
            for k in counts:
                RUN[k][4](sp, counts[k])
            for b in range(B):
                x_is(len(counts))(sp, b)
                sp.dma_start(cols(dram["out"], b), cols(x, b)).then_inc(stored, 16)
            sp.wait_ge(stored, 16 * B)
            for s in range(len(SECTIONS)):
                sp.wait_ge(w_loaded[s], 16 * (1 + counts_layers(counts)))


def counts_layers(counts):
    return NL * sum(k in counts for k in (4, 6))


def shape_constants():
    eye = np.eye(P, dtype=np.float32)
    selector = np.zeros((P, P), np.float32)
    for m in range(P):
        selector[32 * (m // 32) + HD, m] = 1.0
    consts = np.concatenate([eye - np.float32(1 / P), np.full((P, P), 1 / P, np.float32), selector, eye], axis=1)
    half = HD // 2
    inv = (1.0 / np.float32(10000.0) ** (np.arange(half, dtype=np.float32) / np.float32(half))).astype(np.float32)
    ang = np.arange(S, dtype=np.float32)[:, None] * inv
    rope = np.zeros((P, 2, S), np.float32)
    for r in range(P):
        i = r // H
        rope[r, 0] = np.cos(ang[:, i % half])
        rope[r, 1] = np.sin(ang[:, i % half]) * (-1 if i < half else 1)
    return {"consts": consts, "rope": rope}


def lay_out(inp):
    t = lambda a: np.ascontiguousarray(np.swapaxes(a, -1, -2))
    order = np.array([hd * HD + i for i in range(HD) for hd in range(H)])
    partner = np.array([hd * HD + (i + HD // 2) % HD for i in range(HD) for hd in range(H)])

    def spread(wt):
        out = np.zeros((P, GROUPS, D), wt.dtype)
        for g in range(GROUPS):
            for j in range(HG):
                out[32 * j:32 * j + HD, g] = wt[(g * HG + j) * HD:(g * HG + j + 1) * HD]
        return out.reshape(P, GROUPS * D)

    weights, biases = [], []
    for s in ("L2_xcond_", "L3_xcond_"):
        g = {k: inp[s + k] for k in ("n1_w", "n1_b", "n2_w", "n2_b", "n3_w", "n3_b", "qkv_w", "so_w", "cq_w", "ck_w",
                                     "cv_w", "co_w", "f1_w", "f1_b", "f2_w", "f2_b")}
        for i in range(NL):
            q, k, v = (g["qkv_w"][i][D * j:D * (j + 1)] for j in range(3))
            cq, ck, cv = (g[n][i] for n in ("cq_w", "ck_w", "cv_w"))
            weights.append(np.concatenate(
                [t(g[n][i]) for n in ("n1_w", "n2_w", "n3_w")]
                + [t(q)[:, order], t(q)[:, partner], t(k)[:, order], t(k)[:, partner], t(v)]
                + [t(cq)[:, order], t(cq)[:, partner], t(ck)[:, order], t(ck)[:, partner], t(cv)]
                + [spread(t(g["so_w"][i])), spread(t(g["co_w"][i])), t(g["f1_w"][i]),
                   t(g["f2_w"][i]).reshape(FT, P, D).transpose(1, 0, 2).reshape(P, DFF)], axis=1))
            biases.append(np.concatenate(
                [g[n][i].reshape(2, D) for n in ("n1_b", "n2_b", "n3_b")]
                + [g["f1_b"][i].reshape(FT, P), g["f2_b"][i].reshape(1, D)], axis=0))
    weights.append(weights[-1])
    moe = lambda pre, n, w1, w2, b1, b2: np.concatenate([np.concatenate(
        [w1(e), w2(e).reshape(FT, P, D).transpose(1, 0, 2).reshape(P, DFF),
         np.where(np.arange(P)[:, None] == e, np.float32(1), np.float32(0)) * np.ones((1, P), np.float32), b1(e), b2(e)],
        axis=1) for e in range(n)], axis=0)
    none = np.zeros((P, FT), np.float32)
    pre = "L3_ffn_"
    rep = lambda a, n: np.ascontiguousarray(np.broadcast_to(a.reshape(1, -1), (n, a.size)))
    z = "L0_xcond_"
    low_a, low_b = inp["L1_ffn_lora_A"], inp["L1_ffn_lora_B"]
    ER = low_a.shape[0] * low_a.shape[1]
    wa3, wb3, spread3 = np.zeros((P, P), np.float32), np.zeros((P, DFF), np.float32), np.zeros((8, P), np.float32)
    wa3[:, :ER] = t(low_a.reshape(ER, D))
    wb3[:ER] = low_b.transpose(0, 2, 1).reshape(ER, DFF)
    for e in range(8):
        spread3[e, 4 * e:4 * e + 4] = 1.0
    other = {
        "w0": np.concatenate([inp[z + k] for k in ("wk", "wv", "wq", "wu", "w1", "w2")], axis=1),
        "vec0": t(np.concatenate([inp[z + k].reshape(1, D) for k in (
            "q_mu", "q_logsig", "lnkv_g", "lnkv_b", "lnq_g", "lnq_b", "lnm_g", "lnm_b", "lnp_g", "lnp_b", "bk", "bq",
            "bu", "b1", "b2")], axis=0)),
        "bv_rows": rep(inp[z + "bv"], P),
        "rw1": t(inp["L0_ffn_router_w"]), "iota8": rep(np.arange(8, dtype=np.float32), P),
        "we1": moe("", 8, lambda e: t(inp["L0_ffn_expert_w1"][e]), lambda e: t(inp["L0_ffn_expert_w2"][e]),
                   lambda e: none, lambda e: none[:, 0:1]),
        "we3": moe("", 16, lambda e: inp[pre + "w1"][e], lambda e: inp[pre + "w2"][e],
                   lambda e: t(inp[pre + "b1"][e].reshape(FT, P)), lambda e: inp[pre + "b2"][e].reshape(D, 1)),
        "heads2": np.concatenate([np.concatenate(
            [t(inp["L1_xcond_Wq"][64 * i:64 * i + 64]), t(inp["L1_xcond_Wkv"][64 * i:64 * i + 64]),
             t(inp["L1_xcond_Wkv"][1024 + 64 * i:1024 + 64 * i + 64]),
             np.concatenate([t(inp["L1_xcond_Wo"][:, 64 * i:64 * i + 64]), np.zeros((64, D), np.float32)], axis=0)],
            axis=1) for i in range(16)], axis=0),
        "vec2": t(np.concatenate([inp["L1_xcond_" + k].reshape(1, D) for k in ("ln1_w", "ln1_b", "ln2_w", "ln2_b")],
                                 axis=0)),
        "rw3": t(inp["L1_ffn_gate_W"]), "rb3": rep(inp["L1_ffn_gate_b"], P), "wa3": wa3, "wb3": wb3,
        "wi3": t(inp["L1_ffn_wi_W"]), "wo3": t(inp["L1_ffn_wo_W"]).reshape(FT, P, D).transpose(1, 0, 2).reshape(P, DFF),
        "spread3": spread3,
        "vec3": t(np.concatenate([inp["L1_ffn_wi_b"].reshape(FT, P), inp["L1_ffn_wo_b"].reshape(1, D)], axis=0)),
        "wg5": inp["L2_ffn_w_gate"], "wu5": inp["L2_ffn_w_up"], "wd5": inp["L2_ffn_w_down"],
        "gq7": t(inp["L3_ffn_gate_query"]), "temp7": np.ascontiguousarray(rep(inp["L3_ffn_log_temp"], 16)),
    }
    masks = np.concatenate([inp["mask_BxS_bf0"], inp["mask_BxS2_bf0"], np.zeros((B, MASK_BYTES - S - CTX), bool)],
                           axis=1).view(np.uint32)
    out = {
        "x": t(inp["x"].reshape(T, D)), "ctx": t(inp["ctx_1024"].reshape(B * CTX, D)), "cond": t(inp["cond_1024"]),
        "masks": masks, "weights": np.concatenate(weights, axis=0),
        "biases": t(np.concatenate(biases, axis=0)), **shape_constants(), **other,
    }
    return {k: np.ascontiguousarray(v) for k, v in out.items()}


def kernel(**inputs):
    import concourse.bacc as bacc
    from concourse.bass_utils import run_bass_kernel_spmd

    arrays = lay_out({k: np.asarray(v) for k, v in inputs.items()})
    nc = bacc.Bacc("TRN2", target_bir_lowering=False, num_devices=1)
    dram = {k: nc.dram_tensor(k + "_dram", v.shape, mybir.dt.from_np(v.dtype), kind="ExternalInput").ap()
            for k, v in arrays.items()}
    dram["out"] = nc.dram_tensor("out_dram", [P, T], F32, kind="ExternalOutput").ap()
    build(nc, dram)
    r = run_bass_kernel_spmd(nc, [{k + "_dram": v for k, v in arrays.items()}], core_ids=[0])
    return np.ascontiguousarray(r.results[0]["out_dram"].T).reshape(B, S, D)
```
